# Optimizing a Trainium2 kernel written in Bass

```python
import numpy as np
import jax
import jax.numpy as jnp

def _softmax(x, axis=-1):
    return jax.nn.softmax(x, axis=axis)

def _gelu(x):
    return jax.nn.gelu(x, approximate=True)

def _silu(x):
    return jax.nn.silu(x)

def _sigmoid(x):
    return jax.nn.sigmoid(x)

def _layernorm(x, axis=-1, eps=1e-05):
    m = jnp.mean(x, axis=axis, keepdims=True)
    v = jnp.var(x, axis=axis, keepdims=True)
    return (x - m) / jnp.sqrt(v + eps)

def _scatter_add(tgt, idx, src, axis=0):
    return tgt.at[idx].add(src)

def _segment_sum(src, seg, n):
    return jax.ops.segment_sum(src, seg, n)
kernel_name = 'mk_dlrm_tower_d1_rec_r8_98f66c'

def setup_inputs(seed: int=0):
    np.random.seed(seed)
    _w = jnp.asarray

    def _rec_inputs():
        import jax
        import jax.numpy as jnp
        _tk = jax.random.key(seed)
        ids = jnp.stack([jax.random.randint(jax.random.fold_in(_tk, 200 + f), (512,), 0, v, jnp.int32) for f, v in enumerate([1000, 1250, 1000, 1250, 125000, 1250, 1250, 125000, 125000, 1250, 1000, 12500, 1000, 1250, 1000, 1250, 1250, 12500, 1250, 1250, 1250, 1000, 1250, 1000, 1250, 1000])], axis=1)
        tbl_0 = 0.05 * jax.random.normal(jax.random.fold_in(_tk, 500 + 0), (1000, 64), jnp.float32)
        tbl_1 = 0.05 * jax.random.normal(jax.random.fold_in(_tk, 500 + 1), (1250, 64), jnp.float32)
        tbl_2 = 0.05 * jax.random.normal(jax.random.fold_in(_tk, 500 + 2), (1000, 64), jnp.float32)
        tbl_3 = 0.05 * jax.random.normal(jax.random.fold_in(_tk, 500 + 3), (1250, 64), jnp.float32)
        tbl_4 = 0.05 * jax.random.normal(jax.random.fold_in(_tk, 500 + 4), (125000, 64), jnp.float32)
        tbl_5 = 0.05 * jax.random.normal(jax.random.fold_in(_tk, 500 + 5), (1250, 64), jnp.float32)
        tbl_6 = 0.05 * jax.random.normal(jax.random.fold_in(_tk, 500 + 6), (1250, 64), jnp.float32)
        tbl_7 = 0.05 * jax.random.normal(jax.random.fold_in(_tk, 500 + 7), (125000, 64), jnp.float32)
        tbl_8 = 0.05 * jax.random.normal(jax.random.fold_in(_tk, 500 + 8), (125000, 64), jnp.float32)
        tbl_9 = 0.05 * jax.random.normal(jax.random.fold_in(_tk, 500 + 9), (1250, 64), jnp.float32)
        tbl_10 = 0.05 * jax.random.normal(jax.random.fold_in(_tk, 500 + 10), (1000, 64), jnp.float32)
        tbl_11 = 0.05 * jax.random.normal(jax.random.fold_in(_tk, 500 + 11), (12500, 64), jnp.float32)
        tbl_12 = 0.05 * jax.random.normal(jax.random.fold_in(_tk, 500 + 12), (1000, 64), jnp.float32)
        tbl_13 = 0.05 * jax.random.normal(jax.random.fold_in(_tk, 500 + 13), (1250, 64), jnp.float32)
        tbl_14 = 0.05 * jax.random.normal(jax.random.fold_in(_tk, 500 + 14), (1000, 64), jnp.float32)
        tbl_15 = 0.05 * jax.random.normal(jax.random.fold_in(_tk, 500 + 15), (1250, 64), jnp.float32)
        tbl_16 = 0.05 * jax.random.normal(jax.random.fold_in(_tk, 500 + 16), (1250, 64), jnp.float32)
        tbl_17 = 0.05 * jax.random.normal(jax.random.fold_in(_tk, 500 + 17), (12500, 64), jnp.float32)
        tbl_18 = 0.05 * jax.random.normal(jax.random.fold_in(_tk, 500 + 18), (1250, 64), jnp.float32)
        tbl_19 = 0.05 * jax.random.normal(jax.random.fold_in(_tk, 500 + 19), (1250, 64), jnp.float32)
        tbl_20 = 0.05 * jax.random.normal(jax.random.fold_in(_tk, 500 + 20), (1250, 64), jnp.float32)
        tbl_21 = 0.05 * jax.random.normal(jax.random.fold_in(_tk, 500 + 21), (1000, 64), jnp.float32)
        tbl_22 = 0.05 * jax.random.normal(jax.random.fold_in(_tk, 500 + 22), (1250, 64), jnp.float32)
        tbl_23 = 0.05 * jax.random.normal(jax.random.fold_in(_tk, 500 + 23), (1000, 64), jnp.float32)
        tbl_24 = 0.05 * jax.random.normal(jax.random.fold_in(_tk, 500 + 24), (1250, 64), jnp.float32)
        tbl_25 = 0.05 * jax.random.normal(jax.random.fold_in(_tk, 500 + 25), (1000, 64), jnp.float32)
        _rk = jax.random.fold_in(_tk, 7)
        r_dense_t = 7.22013e-05 + 1.00017 * jax.random.normal(jax.random.fold_in(_rk, 101), (512, 256), jnp.float32)
        W_top1 = 0.0360844 * jax.random.normal(jax.random.fold_in(_tk, 801), (768, 512), jnp.float32)
        W_top2 = 0.0441942 * jax.random.normal(jax.random.fold_in(_tk, 802), (512, 256), jnp.float32)
        W_top3 = 0.0625 * jax.random.normal(jax.random.fold_in(_tk, 803), (256, 1), jnp.float32)
        b_top1 = jnp.zeros((512,), jnp.float32)
        b_top2 = jnp.zeros((256,), jnp.float32)
        return (r_dense_t, ids, tbl_0, tbl_1, tbl_2, tbl_3, tbl_4, tbl_5, tbl_6, tbl_7, tbl_8, tbl_9, tbl_10, tbl_11, tbl_12, tbl_13, tbl_14, tbl_15, tbl_16, tbl_17, tbl_18, tbl_19, tbl_20, tbl_21, tbl_22, tbl_23, tbl_24, tbl_25, W_top1, b_top1, W_top2, b_top2, W_top3)
    r_dense_t, ids, tbl_0, tbl_1, tbl_2, tbl_3, tbl_4, tbl_5, tbl_6, tbl_7, tbl_8, tbl_9, tbl_10, tbl_11, tbl_12, tbl_13, tbl_14, tbl_15, tbl_16, tbl_17, tbl_18, tbl_19, tbl_20, tbl_21, tbl_22, tbl_23, tbl_24, tbl_25, W_top1, b_top1, W_top2, b_top2, W_top3 = _rec_inputs()

    def _L0_rec_setup():
        import jax, jax.numpy as jnp
        import numpy as np
        EPS = 1e-05
        NI = 33
        TRIL_I, TRIL_J = np.tril_indices(NI, k=-1)

        def layer_norm(x, g, b):
            m = jnp.mean(x, axis=-1, keepdims=True)
            v = jnp.mean(jnp.square(x - m), axis=-1, keepdims=True)
            return (x - m) * jax.lax.rsqrt(v + EPS) * g + b
        key = jax.random.key(seed)
        ks = jax.random.split(key, 8)
        B, D_DENSE, N_SP, D_SP = (4096, 256, 26, 64)
        E, PROJ, MAXD, NFLAT = (128, 32, 512, 528)
        dense_t = jax.random.normal(ks[0], (B, D_DENSE), dtype=jnp.float32)
        sparse_t = jax.random.normal(ks[1], (B, N_SP, D_SP), dtype=jnp.float32)
        Wd = jax.random.normal(ks[2], (E, D_DENSE), dtype=jnp.float32) / np.sqrt(D_DENSE)
        Ws = jax.random.normal(ks[3], (E, D_SP), dtype=jnp.float32) / np.sqrt(D_SP)
        Wsi = jax.random.normal(ks[4], (PROJ, N_SP), dtype=jnp.float32) / np.sqrt(N_SP)
        Wl = jax.random.normal(ks[5], (MAXD, NFLAT), dtype=jnp.float32) / np.sqrt(NFLAT)
        gd = jnp.ones((E,), jnp.float32)
        bd = jnp.zeros((E,), jnp.float32)
        gs = jnp.ones((E,), jnp.float32)
        bs = jnp.zeros((E,), jnp.float32)
        gsi = jnp.ones((PROJ,), jnp.float32)
        bsi = jnp.zeros((PROJ,), jnp.float32)
        gl = jnp.ones((MAXD,), jnp.float32)
        bl = jnp.zeros((MAXD,), jnp.float32)
        return {'dense_t': dense_t, 'sparse_t': sparse_t, 'Wd': Wd, 'gd': gd, 'bd': bd, 'Ws': Ws, 'gs': gs, 'bs': bs, 'Wsi': Wsi, 'gsi': gsi, 'bsi': bsi, 'Wl': Wl, 'gl': gl, 'bl': bl, 'dims_in_use': 384}
    _L0_rec_all = _L0_rec_setup()
    _L0_rec_in = {k: v for k, v in _L0_rec_all.items() if k in ('Wd', 'gd', 'bd', 'Ws', 'gs', 'bs', 'Wsi', 'gsi', 'bsi', 'Wl', 'gl', 'bl')}
    del _L0_rec_all
    return {'r_dense_t': r_dense_t, 'ids': ids, 'tbl_0': tbl_0, 'tbl_1': tbl_1, 'tbl_2': tbl_2, 'tbl_3': tbl_3, 'tbl_4': tbl_4, 'tbl_5': tbl_5, 'tbl_6': tbl_6, 'tbl_7': tbl_7, 'tbl_8': tbl_8, 'tbl_9': tbl_9, 'tbl_10': tbl_10, 'tbl_11': tbl_11, 'tbl_12': tbl_12, 'tbl_13': tbl_13, 'tbl_14': tbl_14, 'tbl_15': tbl_15, 'tbl_16': tbl_16, 'tbl_17': tbl_17, 'tbl_18': tbl_18, 'tbl_19': tbl_19, 'tbl_20': tbl_20, 'tbl_21': tbl_21, 'tbl_22': tbl_22, 'tbl_23': tbl_23, 'tbl_24': tbl_24, 'tbl_25': tbl_25, 'W_top1': W_top1, 'b_top1': b_top1, 'W_top2': W_top2, 'b_top2': b_top2, 'W_top3': W_top3, 'L0_rec_Wd': _L0_rec_in['Wd'], 'L0_rec_gd': _L0_rec_in['gd'], 'L0_rec_bd': _L0_rec_in['bd'], 'L0_rec_Ws': _L0_rec_in['Ws'], 'L0_rec_gs': _L0_rec_in['gs'], 'L0_rec_bs': _L0_rec_in['bs'], 'L0_rec_Wsi': _L0_rec_in['Wsi'], 'L0_rec_gsi': _L0_rec_in['gsi'], 'L0_rec_bsi': _L0_rec_in['bsi'], 'L0_rec_Wl': _L0_rec_in['Wl'], 'L0_rec_gl': _L0_rec_in['gl'], 'L0_rec_bl': _L0_rec_in['bl']}

def reference(r_dense_t, ids, tbl_0, tbl_1, tbl_2, tbl_3, tbl_4, tbl_5, tbl_6, tbl_7, tbl_8, tbl_9, tbl_10, tbl_11, tbl_12, tbl_13, tbl_14, tbl_15, tbl_16, tbl_17, tbl_18, tbl_19, tbl_20, tbl_21, tbl_22, tbl_23, tbl_24, tbl_25, W_top1, b_top1, W_top2, b_top2, W_top3, L0_rec_Wd, L0_rec_gd, L0_rec_bd, L0_rec_Ws, L0_rec_gs, L0_rec_bs, L0_rec_Wsi, L0_rec_gsi, L0_rec_bsi, L0_rec_Wl, L0_rec_gl, L0_rec_bl):
    import jax
    import jax.numpy as jnp

    def _L0_rec_ref(dense_t, sparse_t, Wd, gd, bd, Ws, gs, bs, Wsi, gsi, bsi, Wl, gl, bl, dims_in_use):
        import jax, jax.numpy as jnp
        import numpy as np
        EPS = 1e-05
        NI = 33
        TRIL_I, TRIL_J = np.tril_indices(NI, k=-1)

        def layer_norm(x, g, b):
            m = jnp.mean(x, axis=-1, keepdims=True)
            v = jnp.mean(jnp.square(x - m), axis=-1, keepdims=True)
            return (x - m) * jax.lax.rsqrt(v + EPS) * g + b
        x = layer_norm(dense_t @ Wd.T, gd, bd)
        y = layer_norm(jnp.einsum('bnd,ed->bne', sparse_t, Ws), gs, bs)
        y = jnp.einsum('bne,pn->bep', y, Wsi)
        y = layer_norm(y, gsi, bsi)
        y = jnp.swapaxes(y, 1, 2)
        T = jnp.concatenate([x[:, None, :], y], axis=1)
        Z = jnp.einsum('bnd,bmd->bnm', T, T)
        Zflat = Z[:, TRIL_I, TRIL_J]
        out = layer_norm(Zflat @ Wl.T, gl, bl)
        maxd = out.shape[-1]
        mask = (jnp.arange(maxd) < dims_in_use).astype(out.dtype)
        return out * mask
    e = jnp.stack([tbl_0[ids[:, 0]], tbl_1[ids[:, 1]], tbl_2[ids[:, 2]], tbl_3[ids[:, 3]], tbl_4[ids[:, 4]], tbl_5[ids[:, 5]], tbl_6[ids[:, 6]], tbl_7[ids[:, 7]], tbl_8[ids[:, 8]], tbl_9[ids[:, 9]], tbl_10[ids[:, 10]], tbl_11[ids[:, 11]], tbl_12[ids[:, 12]], tbl_13[ids[:, 13]], tbl_14[ids[:, 14]], tbl_15[ids[:, 15]], tbl_16[ids[:, 16]], tbl_17[ids[:, 17]], tbl_18[ids[:, 18]], tbl_19[ids[:, 19]], tbl_20[ids[:, 20]], tbl_21[ids[:, 21]], tbl_22[ids[:, 22]], tbl_23[ids[:, 23]], tbl_24[ids[:, 24]], tbl_25[ids[:, 25]]], axis=1)
    z = _L0_rec_ref(r_dense_t, e, L0_rec_Wd, L0_rec_gd, L0_rec_bd, L0_rec_Ws, L0_rec_gs, L0_rec_bs, L0_rec_Wsi, L0_rec_gsi, L0_rec_bsi, L0_rec_Wl, L0_rec_gl, L0_rec_bl, 384)
    z = z.reshape(z.shape[0], -1)
    h = jnp.concatenate([z, r_dense_t], axis=1)
    h = jnp.maximum(h @ W_top1 + b_top1, 0.0)
    h = jnp.maximum(h @ W_top2 + b_top2, 0.0)
    y = h @ W_top3
    return y

_drawn_inputs = setup_inputs


def setup_inputs(seed=0):
    import zlib

    import numpy as np

    out = dict(_drawn_inputs(seed))
    spreads = {'b_top1': (0.0, 0.1),
     'b_top2': (0.0, 0.1),
     'L0_rec_gd': (1.0, 0.6),
     'L0_rec_bd': (0.0, 0.8),
     'L0_rec_gs': (1.0, 0.6),
     'L0_rec_bs': (0.0, 0.1),
     'L0_rec_gsi': (1.0, 0.2),
     'L0_rec_bsi': (0.0, 0.1),
     'L0_rec_gl': (1.0, 0.2),
     'L0_rec_bl': (0.0, 0.1)}
    factors = {}
    for name, (base, spread) in spreads.items():
        noise = np.random.default_rng([zlib.crc32(name.encode()), seed]).standard_normal(out[name].shape)
        drawn = base * np.exp(spread * noise) if base else spread * noise
        out[name] = jnp.asarray(drawn.astype(out[name].dtype))
    for name, factor in factors.items():
        out[name] = (out[name] * factor).astype(out[name].dtype)
    return out
```

```python
from contextlib import ExitStack

import numpy as np

import concourse.bass as bass
from concourse import mybir

B = 512
NF = 26
D = 64
E = 128
P = 32
MAXD, USED = 512, 384
DD = 256
H1, H2 = 512, 256
EPS = 1e-5

BT = 128
ROUNDS = B // BT
TILES = BT * NF // 128
GT = 4
GROUPS = -(-TILES // GT)
BANK_B = 16
BANKS = BT // BANK_B
PATTERN = 13
PATTERN_B = PATTERN * 128 // NF
BLK = 6
CHUNKS = 5
HALF = BT // 2
TOPK = (USED + DD) // 128


def group_tiles(q):
    return list(range(GT * q, min(GT * q + GT, TILES)))


def bank_parts(m):
    mm, base = m % (BANKS // 2), PATTERN * (m // (BANKS // 2))
    parts = []
    for tt in range(BANK_B * NF * mm // 128, (BANK_B * NF * (mm + 1) - 1) // 128 + 1):
        first, last = 128 * tt // NF, (128 * tt + 127) // NF
        lo, hi = max(first, BANK_B * mm), min(last, BANK_B * mm + BANK_B - 1)
        parts.append((base + tt, tt, P * (lo - BANK_B * mm), P * (hi + 1 - BANK_B * mm), lo - first, hi + 1 - first))
    return parts


def bank_group(m):
    return bank_parts(m)[-1][0] // GT


def last_bank(q):
    return max(m for m in range(BANKS) if any(p[0] in group_tiles(q) for p in bank_parts(m)))


VEC = {}
for _name, _n in (("gs", 1), ("gd", 1), ("bd", 1), ("gl", USED // 128), ("bl", USED // 128), ("b1", H1 // 128),
                  ("b2", H2 // 128), ("w3", H2 // 128), ("gsi", P), ("bsi", P)):
    VEC[_name] = (sum(n for _, n in VEC.values()), _n)
NVEC = sum(n for _, n in VEC.values())


def dlrm_tower(nc, tbl, ids, base, ident, vecs, bs_row, ws_t, wsi_blocks, dense_t, wd_t, wl_chunks, w1, w2, out):
    fp32, i32 = mybir.dt.float32, mybir.dt.int32
    ALU, ACT, AX = mybir.AluOpType, mybir.ActivationFunctionType, mybir.AxisListType

    ctx = ExitStack()
    with ctx:
        def sb(name, shape, dt=fp32):
            return ctx.enter_context(nc.sbuf_tensor(name, shape, dt))

        def ps(name, shape):
            return ctx.enter_context(nc.psum_tensor(name, shape, fp32))

        def sem(name):
            return ctx.enter_context(nc.semaphore(name))

        idx = sb("idx", [128, ROUNDS * TILES], i32)
        idx_base = sb("idx_base", [128, ROUNDS * TILES], i32)
        identity = sb("identity", [128, 128])
        vec = sb("vec", [128, NVEC])
        bs_rep = sb("bs_rep", [NF, E])
        ws_raw = sb("ws_raw", [128, E])
        ws_mean = sb("ws_mean", [128, 1])
        ws_diag = sb("ws_diag", [128, 2, E])
        wsi = sb("wsi", [128, PATTERN, BLK, P])
        wsi_mean = sb("wsi_mean", [128, PATTERN * BLK])
        shift = sb("shift", [128, P])
        dense = sb("dense", [128, DD // 128, B])
        wd = sb("wd", [128, DD // 128, E])
        wl = sb("wl", [128, CHUNKS, MAXD])
        w_top1 = sb("w_top1", [128, TOPK, H1])
        w_top2 = sb("w_top2", [128, H1 // 128, H2])
        eps = sb("eps", [128, 1])

        def col(name, k=0, n=1):
            at = VEC[name][0] + k
            return vec[:, at:at + n]

        xn = sb("xn", [128, 2, E])
        x_t = sb("x_t", [128, B])
        emb = sb("emb", [128, TILES, D])
        emb_t = sb("emb_t", [128, 2, 2, 128])
        u_sq = sb("u_sq", [128, 2, GT, E])
        u_var = sb("u_var", [128, 2, GT])
        u_std = sb("u_std", [128, 2, GT])
        u_rstd = sb("u_rstd", [128, 2, GT])
        u_norm = sb("u_norm", [128, TILES, E])
        y = sb("y", [128, 2, BANK_B, P])
        y_sq = sb("y_sq", [128, 2, BANK_B, P])
        y_var = sb("y_var", [128, 2, BANK_B])
        y_std = sb("y_std", [128, 2, BANK_B])
        y_rstd = sb("y_rstd", [128, 2, BANK_B])
        rows = sb("rows", [128, 2, P + 1, HALF])
        z = sb("z", [128, P, P])
        z_pack = sb("z_pack", [128, CHUNKS, 128])
        z_t = sb("z_t", [128, CHUNKS, BT])
        stats = sb("stats", [128, 6])
        mean_var = sb("mean_var", [128, 2])
        carrier = sb("carrier", [128, 7])
        l_std = sb("l_std", [128, 1])
        l_rstd = sb("l_rstd", [128, 1])
        l_norm = sb("l_norm", [128, USED])
        l_t = sb("l_t", [128, USED // 128, BT])
        h1 = sb("h1", [128, H1 // 128, BT])
        h2 = sb("h2", [128, H2 // 128, BT])
        y_out = sb("y_out", [1, B])

        ps_t = ps("ps_t", [128, 512])
        ps_u = [ps(f"ps_u{i}", [128, GT, E]) for i in range(2)]
        ps_y = [ps(f"ps_y{i}", [128, BANK_B, P]) for i in range(2)]
        ps_z = ps("ps_z", [128, BANK_B * 2, P])
        ps_p = ps("ps_p", [128, 512])

        ids_in, base_in, ident_in, vec_in, bs_in = (sem(n) for n in ("ids_in", "base_in", "ident_in", "vec_in", "bs_in"))
        ws_in, wsi_in, dense_in, wd_in = (sem(n) for n in ("ws_in", "wsi_in", "dense_in", "wd_in"))
        wl_in, w1_in, w2_in = (sem(n) for n in ("wl_in", "w1_in", "w2_in"))
        idx_ready = sem("idx_ready")
        gathered = [sem(f"gathered{q}") for q in range(GROUPS)]
        filled = sem("filled")
        ws_step, wsi_step = sem("ws_step"), sem("wsi_step")
        shift_mm, shift_ready = sem("shift_mm"), sem("shift_ready")
        x_mm, x_stat, x_aggr, x_root, x_inv, x_norm, x_tr, x_ready = (
            sem(n) for n in ("x_mm", "x_stat", "x_aggr", "x_root", "x_inv", "x_norm", "x_tr", "x_ready"))
        emb_turned, emb_copied = sem("emb_turned"), sem("emb_copied")
        u_mm, u_squared, u_summed, u_root, u_inv, u_scaled = (
            sem(n) for n in ("u_mm", "u_squared", "u_summed", "u_root", "u_inv", "u_scaled"))
        y_mm, y_shifted, y_squared, y_summed, y_root, y_inv, y_scaled = (
            sem(n) for n in ("y_mm", "y_shifted", "y_squared", "y_summed", "y_root", "y_inv", "y_scaled"))
        x_placed, rows_ready, z_mm, z_ready, z_packed = (
            sem(n) for n in ("x_placed", "rows_ready", "z_mm", "z_ready", "z_packed"))
        z_turned, zt_copied, l_mm, l_stat, l_aggr, l_root, l_inv, l_scaled, l_turned, lt_ready = (
            sem(n) for n in ("z_turned", "zt_copied", "l_mm", "l_stat", "l_aggr", "l_root", "l_inv", "l_scaled",
                             "l_turned", "lt_ready"))
        h1_mm, h1_ready, h2_mm, h2_ready, out_mm, out_copied, stored = (
            sem(n) for n in ("h1_mm", "h1_ready", "h2_mm", "h2_ready", "out_mm", "out_copied", "stored"))

        def live(t):
            return not isinstance(t[0], int) or 0 <= t[0] + t[1] < ROUNDS

        def count(per_round, t, n):
            return t[0] * per_round + (t[1] * per_round + n)

        def past(per_round, t, n):
            return count(per_round, t, n + 1)

        def wait(eng, s, n):
            if not isinstance(n, int) or n > 0:
                eng.wait_ge(s, n)

        def at(t, q, lag):
            return (t[0], t[1] + (q - lag) // GROUPS), (q - lag) % GROUPS

        def freed(q):
            return q - 1 if q >= 1 else 0

        def run(eng, step):
            for q in range(GROUPS):
                step((0, 0), q)
            with eng.Fori(1, ROUNDS) as t:
                for q in range(GROUPS):
                    step((t, 0), q)
            for q in range(GROUPS):
                step((ROUNDS, 0), q)

        block = ctx.enter_context(nc.Block())

        @block.sync
        def _(sp):
            sp.dma_start(idx[:, :], ids).then_inc(ids_in, 16)
            sp.dma_start(idx_base[:, :], base).then_inc(base_in, 16)
            sp.dma_start(ws_raw[:, :], ws_t).then_inc(ws_in, 16)
            sp.dma_start(identity[:, :], ident).then_inc(ident_in, 16)
            sp.dma_start(vec[:, :], vecs).then_inc(vec_in, 16)
            sp.dma_start(bs_rep[:, :], bs_row).then_inc(bs_in, 16)
            sp.dma_start(wsi[:, :, :, :], wsi_blocks).then_inc(wsi_in, 16)
            sp.dma_start(wd[:, :, :], wd_t).then_inc(wd_in, 16)
            sp.dma_start(dense[:, :, :], dense_t).then_inc(dense_in, 16)
            sp.dma_start(wl[:, :, :], wl_chunks).then_inc(wl_in, 16)
            sp.dma_start(w_top1[:, :, :], w1).then_inc(w1_in, 16)
            sp.dma_start(w_top2[:, :, :], w2).then_inc(w2_in, 16)
            sp.wait_ge(out_copied, ROUNDS + 1)
            sp.dma_start(out, y_out[:, :]).then_inc(stored, 16)
            sp.wait_ge(stored, 16)

        @block.gpsimd
        def _(pool):
            pool.wait_ge(idx_ready, 1)
            for t in range(ROUNDS):
                for q in range(GROUPS):
                    wait(pool, emb_turned, GROUPS * (t - 1) + q + 1)
                    for k in group_tiles(q):
                        g = TILES * t + k
                        pool.indirect_dma_start(
                            emb[:, k, :], None, tbl, bass.IndirectOffsetOnAxis(ap=idx[:, g:g + 1], axis=0),
                        ).then_inc(gathered[q], 16)

        @block.tensor
        def _(pe):
            pe.wait_ge(dense_in, 16)
            pe.wait_ge(wd_in, 16)
            pe.wait_ge(ident_in, 16)
            for r in range(ROUNDS):
                wait(pe, x_ready, r)
                for k in range(DD // 128):
                    mm = nc.tensor.matmul(ps_p[:, 0:E], dense[:, k, BT * r:BT * (r + 1)], wd[:, k, :],
                                          start=(k == 0), stop=(k == DD // 128 - 1))
                mm.then_inc(x_mm, 1)
                pe.wait_ge(x_norm, r + 1)
                nc.tensor.transpose(ps_p[:, 0:BT], xn[:, r % 2, :], identity[:, :]).then_inc(x_tr, 1)
            pe.wait_ge(x_ready, ROUNDS)
            pe.wait_ge(bs_in, 16)
            pe.wait_ge(wsi_step, 2)
            nc.tensor.matmul(ps_p[:, 0:P], bs_rep[:, :], wsi[0:NF, 0, 0, :], start=True, stop=True).then_inc(shift_mm, 1)

            def turn_gathers(t, q):
                pe.wait_ge(gathered[q], count(16 * len(group_tiles(q)), t, 16 * len(group_tiles(q))))
                wait(pe, emb_copied, count(GROUPS, t, q))
                for i, k in enumerate(group_tiles(q)[::2]):
                    mm = nc.tensor.transpose(ps_t[:, 128 * i:128 * (i + 1)],
                                             emb[:, k:k + 2, :].rearrange("p k d -> p (k d)"), identity[:, :])
                mm.then_inc(emb_turned, 1)

            def project(t, q):
                pe.wait_ge(emb_copied, count(GROUPS, t, q + 1))
                wait(pe, u_scaled, count(GROUPS, t, freed(q)))
                for i in range(len(group_tiles(q)) // 2):
                    mm = nc.tensor.matmul(ps_u[q % 2][:, 2 * i:2 * i + 2, :], emb_t[:, q % 2, i, :], ws_diag[:, :, :],
                                          start=True, stop=True)
                mm.then_inc(u_mm, 1)

            def mix_features(t, m):
                pe.wait_ge(u_scaled, count(GROUPS, t, bank_group(m) + 1))
                wait(pe, y_shifted, count(BANKS, t, m - 1))
                parts = bank_parts(m)
                flat = ps_y[m % 2][:, :, :].rearrange("p b r -> p (b r)")
                for n, (tile, tt, lo, hi, b0, b1) in enumerate(parts):
                    mm = nc.tensor.matmul(flat[:, lo:hi], u_norm[:, tile, :], wsi[:, tt, b0:b1, :],
                                          start=(n == 0), stop=(n == len(parts) - 1), skip_group_check=True)
                mm.then_inc(y_mm, 1)

            def pairs(t, half):
                pe.wait_ge(rows_ready, count(2, t, half + 1))
                pe.wait_ge(x_placed, count(2, t, half + 1))
                if half == 0:
                    wait(pe, z_ready, count(1, t, 0))
                for b in range(HALF):
                    quarter, bb = 2 * half + b // 32, b % 32
                    mm = nc.tensor.matmul(ps_z[32 * quarter:32 * quarter + 32, bb, :], rows[:, half, 1:P + 1, b],
                                          rows[:, half, 0:P, b], start=True, stop=True)
                mm.then_inc(z_mm, 1)

            def turn_pairs(t, chunks):
                if chunks[0] == 0:
                    pe.wait_ge(z_packed, past(1, t, 1))
                    wait(pe, out_copied, past(1, t, 0))
                else:
                    pe.wait_ge(zt_copied, count(2, t, 1))
                for i, c in enumerate(chunks):
                    mm = nc.tensor.transpose(ps_p[:, BT * i:BT * (i + 1)], z_pack[:, c, :], identity[:, :])
                mm.then_inc(z_turned, 1)

            def interaction_layer(t):
                pe.wait_ge(zt_copied, count(2, t, 2))
                for c in range(CHUNKS):
                    mm = nc.tensor.matmul(ps_p[:, :], z_t[:, c, :], wl[:, c, :], start=(c == 0), stop=(c == CHUNKS - 1))
                mm.then_inc(l_mm, 1)

            def turn_layer(t):
                pe.wait_ge(l_scaled, count(1, t, 1))
                for c in range(USED // 128):
                    mm = nc.tensor.transpose(ps_p[:, BT * c:BT * (c + 1)], l_norm[:, 128 * c:128 * (c + 1)], identity[:, :])
                mm.then_inc(l_turned, 1)

            def top1(t):
                pe.wait_ge(lt_ready, count(1, t, 1))
                for c in range(H1 // 128):
                    for k in range(TOPK):
                        kd = k - USED // 128
                        rhs = l_t[:, k, :] if kd < 0 else dense[:, kd, bass.ds((t[0] + t[1]) * BT, BT)]
                        mm = nc.tensor.matmul(ps_p[:, BT * c:BT * (c + 1)], w_top1[:, k, 128 * c:128 * (c + 1)], rhs,
                                              start=(k == 0), stop=(k == TOPK - 1))
                mm.then_inc(h1_mm, 1)

            def top2(t):
                pe.wait_ge(h1_ready, count(1, t, 1))
                for c in range(H2 // 128):
                    for k in range(H1 // 128):
                        mm = nc.tensor.matmul(ps_p[:, BT * c:BT * (c + 1)], w_top2[:, k, 128 * c:128 * (c + 1)], h1[:, k, :],
                                              start=(k == 0), stop=(k == H1 // 128 - 1))
                mm.then_inc(h2_mm, 1)

            def top3(t):
                pe.wait_ge(h2_ready, count(1, t, 1))
                for k in range(H2 // 128):
                    mm = nc.tensor.matmul(ps_p[0:1, 0:BT], col("w3", k), h2[:, k, :],
                                          start=(k == 0), stop=(k == H2 // 128 - 1))
                mm.then_inc(out_mm, 1)

            def step(t, q):
                before = (t[0], t[1] - 1)
                if live(t):
                    turn_gathers(t, q)
                if live(before):
                    if q == 4:
                        turn_pairs(before, [4])
                    if q == 6:
                        top1(before)
                tl, ql = at(t, q, 1)
                if live(tl):
                    project(tl, ql)
                if live(before) and q == 6:
                    top2(before)
                tl, ql = at(t, q, 2)
                if live(tl):
                    for m in range(BANKS):
                        if bank_group(m) == ql:
                            mix_features(tl, m)
                if live(t) and q == 6:
                    pairs(t, 0)
                if live(before):
                    if q == 2:
                        pairs(before, 1)
                    if q == 3:
                        turn_pairs(before, [0, 1, 2, 3])
                    if q == 4:
                        interaction_layer(before)
                    if q == 5:
                        turn_layer(before)
                    if q == 6:
                        top3(before)

            pe.wait_ge(ws_step, 3)
            pe.wait_ge(shift_ready, 1)
            pe.wait_ge(wl_in, 16)
            pe.wait_ge(w1_in, 16)
            pe.wait_ge(w2_in, 16)
            pe.wait_ge(vec_in, 16)
            run(pe, step)

        @block.scalar
        def _(act):
            act.wait_ge(filled, 1)
            act.wait_ge(vec_in, 16)
            for r in range(ROUNDS):
                act.wait_ge(x_aggr, r + 1)
                nc.scalar.activation(l_std[:, :], mean_var[:, 1:2], ACT.Sqrt, bias=eps[:, :]).then_inc(x_root, 1)
                act.wait_ge(x_tr, r + 1)
                nc.scalar.activation(x_t[:, BT * r:BT * (r + 1)], ps_p[:, 0:BT], ACT.Identity, bias=col("bd"),
                                     scale=col("gd")).then_inc(x_ready, 1)
            act.wait_ge(shift_mm, 1)
            nc.scalar.copy(shift[:, :], ps_p[:, 0:P]).then_inc(shift_ready, 1)

            def copy_gathers(t, q):
                n = len(group_tiles(q)) // 2
                act.wait_ge(emb_turned, count(GROUPS, t, q + 1))
                wait(act, u_mm, count(GROUPS, t, freed(q)))
                nc.scalar.copy(emb_t[:, q % 2, 0:n, :], ps_t[:, 0:128 * n].rearrange("p (n i) -> p n i", n=n)).then_inc(emb_copied, 1)

            def square_u(t, q):
                n = len(group_tiles(q))
                act.wait_ge(u_mm, count(GROUPS, t, q + 1))
                wait(act, u_summed, count(GROUPS, t, freed(q)))
                nc.scalar.activation(u_sq[:, q % 2, 0:n, :], ps_u[q % 2][:, 0:n, :], ACT.Square).then_inc(u_squared, 1)

            def root_u(t, q):
                n = len(group_tiles(q))
                act.wait_ge(u_summed, count(GROUPS, t, q + 1))
                wait(act, u_inv, count(GROUPS, t, freed(q)))
                nc.scalar.activation(u_std[:, q % 2, 0:n], u_var[:, q % 2, 0:n], ACT.Sqrt, bias=eps[:, :],
                                     scale=1.0 / E).then_inc(u_root, 1)

            def square_y(t, m):
                act.wait_ge(y_shifted, count(BANKS, t, m + 1))
                wait(act, y_summed, count(BANKS, t, m - 1))
                nc.scalar.activation(y_sq[:, m % 2, :, :], y[:, m % 2, :, :], ACT.Square).then_inc(y_squared, 1)

            def root_y(t, m):
                act.wait_ge(y_summed, count(BANKS, t, m + 1))
                wait(act, y_inv, count(BANKS, t, m - 1))
                nc.scalar.activation(y_std[:, m % 2, :], y_var[:, m % 2, :], ACT.Sqrt, bias=eps[:, :],
                                     scale=1.0 / P).then_inc(y_root, 1)

            def place_x(t, half):
                wait(act, z_mm, past(2, t, half - 1))
                nc.scalar.copy(rows[:, half, 0, :], x_t[:, bass.ds((t[0] + t[1]) * BT + HALF * half, HALF)]).then_inc(x_placed, 1)

            def copy_pairs(t, n):
                act.wait_ge(z_turned, past(2, t, n + 1))
                wait(act, l_mm, past(1, t, 0))
                c, k = (0, 4) if n == 0 else (4, 1)
                nc.scalar.copy(z_t[:, c:c + k, :], ps_p[:, 0:BT * k].rearrange("p (k b) -> p k b", k=k)).then_inc(zt_copied, 1)

            def root_l(t):
                act.wait_ge(l_aggr, count(1, t, 1))
                nc.scalar.activation(l_std[:, :], mean_var[:, 1:2], ACT.Sqrt, bias=eps[:, :]).then_inc(l_root, 1)

            def scale_l(t):
                act.wait_ge(l_turned, count(1, t, 1))
                for c in range(USED // 128):
                    a = nc.scalar.activation(l_t[:, c, :], ps_p[:, BT * c:BT * (c + 1)], ACT.Identity, bias=col("bl", c),
                                             scale=col("gl", c))
                a.then_inc(lt_ready, 1)

            def relu1(t):
                act.wait_ge(h1_mm, count(1, t, 1))
                for c in range(H1 // 128):
                    a = nc.scalar.activation(h1[:, c, :], ps_p[:, BT * c:BT * (c + 1)], ACT.Relu, bias=col("b1", c))
                a.then_inc(h1_ready, 1)

            def relu2(t):
                act.wait_ge(h2_mm, count(1, t, 1))
                for c in range(H2 // 128):
                    a = nc.scalar.activation(h2[:, c, :], ps_p[:, BT * c:BT * (c + 1)], ACT.Relu, bias=col("b2", c))
                a.then_inc(h2_ready, 1)

            def copy_out(t):
                act.wait_ge(out_mm, count(1, t, 1))
                nc.scalar.copy(y_out[:, bass.ds((t[0] + t[1]) * BT, BT)], ps_p[0:1, 0:BT]).then_inc(out_copied, 1)

            def step(t, q):
                before = (t[0], t[1] - 1)
                if live(t):
                    copy_gathers(t, q)
                if live(before) and q == 4:
                    copy_pairs(before, 0)
                    copy_pairs(before, 1)
                if live(before) and q == 6:
                    scale_l(before)
                tl, ql = at(t, q, 1)
                if live(tl):
                    square_u(tl, ql)
                if live(before) and q == 6:
                    relu1(before)
                tm, qm = at(t, q, 2)
                banks = [m for m in range(BANKS) if bank_group(m) == qm] if live(tm) else []
                for m in banks:
                    square_y(tm, m)
                if live(tl):
                    root_u(tl, ql)
                for m in banks:
                    root_y(tm, m)
                if live(t) and q == 5:
                    place_x(t, 0)
                if live(before):
                    if q == 1:
                        place_x(before, 1)
                    if q == 5:
                        root_l(before)
                    if q == 6:
                        relu2(before)
                        copy_out(before)

            run(act, step)

        @block.vector
        def _(dve):
            nc.vector.memset(eps[:, :], EPS).then_inc(filled, 1)
            nc.vector.memset(ws_diag[:, :, :], 0.0).then_inc(filled, 1)
            for n, s in enumerate((y_mm, z_mm, z_packed, z_turned, l_mm, out_copied)):
                nc.vector.memset(carrier[:, 1 + n:2 + n], 0.0).then_inc(s, 1)
            dve.wait_ge(ids_in, 16)
            dve.wait_ge(base_in, 16)
            nc.vector.tensor_tensor(idx[:, :], idx[:, :], idx_base[:, :], ALU.add).then_inc(idx_ready, 1)
            dve.wait_ge(ws_in, 16)
            nc.vector.tensor_reduce(ws_mean[:, :], ws_raw[:, :], AX.X, ALU.add).then_inc(ws_step, 1)
            dve.wait_ge(ws_step, 1)
            nc.vector.tensor_scalar(ws_mean[:, :], ws_mean[:, :], 1.0 / E, None, ALU.mult).then_inc(ws_step, 1)
            dve.wait_ge(ws_step, 2)
            dve.wait_ge(filled, 2)
            for half in range(2):
                rows_of = slice(D * half, D * (half + 1))
                c = nc.vector.tensor_scalar(ws_diag[rows_of, half, :], ws_raw[rows_of, :], ws_mean[rows_of, :], None,
                                            ALU.subtract)
            c.then_inc(ws_step, 1)
            dve.wait_ge(wsi_in, 16)
            nc.vector.tensor_reduce(wsi_mean[:, :], wsi[:, :, :, :].rearrange("p t b r -> p (t b) r"), AX.X, ALU.add).then_inc(wsi_step, 1)
            dve.wait_ge(wsi_step, 1)
            blocks = wsi[:, :, :, :].rearrange("p t b r -> p (t b) r")
            nc.vector.scalar_tensor_tensor(blocks, wsi_mean[:, :].unsqueeze(2).broadcast_to([128, PATTERN * BLK, P]),
                                           -1.0 / P, blocks, ALU.mult, ALU.add).then_inc(wsi_step, 1)
            for r in range(ROUNDS):
                dve.wait_ge(x_mm, r + 1)
                nc.vector.bn_stats(stats[:, :], ps_p[:, 0:E]).then_inc(x_stat, 1)
                dve.wait_ge(x_stat, r + 1)
                nc.vector.bn_aggr(mean_var[:, :], stats[:, :]).then_inc(x_aggr, 1)
                dve.wait_ge(x_root, r + 1)
                nc.vector.reciprocal(l_rstd[:, :], l_std[:, :]).then_inc(x_inv, 1)
                dve.wait_ge(x_inv, r + 1)
                nc.vector.tensor_scalar(xn[:, r % 2, :], ps_p[:, 0:E], mean_var[:, 0:1], l_rstd[:, :], ALU.subtract,
                                        ALU.mult).then_inc(x_norm, 1)

            def sum_u(t, q):
                n = len(group_tiles(q))
                dve.wait_ge(u_squared, count(GROUPS, t, q + 1))
                wait(dve, u_root, count(GROUPS, t, freed(q)))
                nc.vector.tensor_reduce(u_var[:, q % 2, 0:n], u_sq[:, q % 2, 0:n, :], AX.X, ALU.add).then_inc(u_summed, 1)

            def scale_u(t, q):
                n, first = len(group_tiles(q)), GT * q
                dve.wait_ge(u_root, count(GROUPS, t, q + 1))
                nc.vector.reciprocal(u_rstd[:, q % 2, 0:n], u_std[:, q % 2, 0:n]).then_inc(u_inv, 1)
                dve.wait_ge(u_inv, count(GROUPS, t, q + 1))
                wait(dve, y_mm, past(BANKS, t, last_bank(q) + 1 - BANKS))
                nc.vector.tensor_tensor(u_norm[:, first:first + n, :], ps_u[q % 2][:, 0:n, :],
                                        u_rstd[:, q % 2, 0:n].unsqueeze(2).broadcast_to([128, n, E]), ALU.mult).then_inc(u_scaled, 1)

            def shift_y(t, m):
                dve.wait_ge(y_mm, past(BANKS, t, m + 1))
                wait(dve, y_scaled, count(BANKS, t, m - 1))
                nc.vector.scalar_tensor_tensor(y[:, m % 2, :, :], ps_y[m % 2][:, :, :], col("gs"),
                                               shift[:, :].unsqueeze(1).broadcast_to([128, BANK_B, P]),
                                               ALU.mult, ALU.add).then_inc(y_shifted, 1)

            def sum_y(t, m):
                dve.wait_ge(y_squared, count(BANKS, t, m + 1))
                wait(dve, y_root, count(BANKS, t, m - 1))
                nc.vector.tensor_reduce(y_var[:, m % 2, :], y_sq[:, m % 2, :, :], AX.X, ALU.add).then_inc(y_summed, 1)

            def scale_y(t, m):
                half, b0 = m // (BANKS // 2), BANK_B * (m % (BANKS // 2))
                dve.wait_ge(y_root, count(BANKS, t, m + 1))
                nc.vector.reciprocal(y_rstd[:, m % 2, :], y_std[:, m % 2, :]).then_inc(y_inv, 1)
                dve.wait_ge(y_inv, count(BANKS, t, m + 1))
                wait(dve, z_mm, past(2, t, half - 1))
                nc.vector.tensor_tensor(rows[:, half, 1:P + 1, b0:b0 + BANK_B].rearrange("e r b -> e b r"),
                                        y[:, m % 2, :, :], y_rstd[:, m % 2, :].unsqueeze(2).broadcast_to([128, BANK_B, P]),
                                        ALU.mult).then_inc(y_scaled, 1)

            def affine_rows(t, half):
                dve.wait_ge(y_scaled, count(BANKS, t, BANKS // 2 * (half + 1)))
                for r in range(P):
                    a = nc.vector.tensor_scalar(rows[:, half, r + 1, :], rows[:, half, r + 1, :], col("gsi", r), col("bsi", r),
                                                ALU.mult, ALU.add)
                a.then_inc(rows_ready, 1)

            def turn_z(t):
                dve.wait_ge(z_mm, past(2, t, 2))
                wait(dve, z_packed, past(1, t, 0))
                nc.vector.transpose(z[:, :, :], ps_z[:, :, :].rearrange("p b j -> p j b")).then_inc(z_ready, 1)
                dve.wait_ge(z_ready, count(1, t, 1))
                wait(dve, z_turned, past(2, t, 0))

                def squares(first, step, n):
                    s = z[:, :, :]
                    return bass.AP(s.tensor, s.offset + first, [list(s.ap[0]), [step, n], [P, 8], [1, 8]])

                def packed(c, n):
                    return z_pack[:, c:c + n, :].rearrange("b c (s j i) -> b (c s) j i", s=2, j=8)

                nc.vector.tensor_copy(z_pack[:, 0:2, :].rearrange("b c (j i) -> b (c j) i", j=8), z[:, 0:16, 16:32])
                nc.vector.tensor_copy(packed(2, 1), squares(8, 16 * P + 16, 2))
                nc.vector.tensor_copy(packed(3, 2), squares(0, 8 * P + 8, 4)).then_inc(z_packed, 1)

            def norm_l(t):
                dve.wait_ge(l_mm, past(1, t, 1))
                nc.vector.bn_stats(stats[:, :], ps_p[:, :]).then_inc(l_stat, 1)
                dve.wait_ge(l_stat, count(1, t, 1))
                nc.vector.memset(carrier[:, 0:1], 0.0)
                nc.vector.bn_aggr(mean_var[:, :], stats[:, :]).then_inc(l_aggr, 1)
                dve.wait_ge(l_root, count(1, t, 1))
                nc.vector.reciprocal(l_rstd[:, :], l_std[:, :]).then_inc(l_inv, 1)
                dve.wait_ge(l_inv, count(1, t, 1))
                nc.vector.tensor_scalar(l_norm[:, :], ps_p[:, 0:USED], mean_var[:, 0:1], l_rstd[:, :], ALU.subtract,
                                        ALU.mult).then_inc(l_scaled, 1)

            def step(t, q):
                before = (t[0], t[1] - 1)
                if live(before) and q == 3:
                    turn_z(before)
                tl, ql = at(t, q, 1)
                if live(tl):
                    sum_u(tl, ql)
                tm, qm = at(t, q, 2)
                banks = [m for m in range(BANKS) if bank_group(m) == qm] if live(tm) else []
                for m in banks:
                    shift_y(tm, m)
                if live(tl):
                    scale_u(tl, ql)
                for m in banks:
                    sum_y(tm, m)
                for m in banks:
                    scale_y(tm, m)
                if live(before) and q == 5:
                    norm_l(before)
                if live(t) and q == 5:
                    affine_rows(t, 0)
                if live(before) and q == 1:
                    affine_rows(before, 1)

            dve.wait_ge(shift_ready, 1)
            dve.wait_ge(vec_in, 16)
            run(dve, step)


def wsi_pattern(wsi):
    out = np.zeros((128, PATTERN, BLK, P), wsi.dtype)
    for tt in range(PATTERN):
        for r in range(128):
            b, n = divmod(128 * tt + r, NF)
            out[r, tt, b - 128 * tt // NF, :] = wsi[:, n]
    return out


def pair_rows():
    of = np.full((CHUNKS, 128), -1)
    for c in range(CHUNKS):
        for k in range(128):
            if c < 2:
                j, i1 = 8 * c + k // 16, 16 + k % 16
            else:
                s, j, i1 = k // 64, k // 8 % 8, k % 8
                if c == 2:
                    j, i1 = j + 16 * s, i1 + 8 + 16 * s
                else:
                    j, i1 = j + 8 * (2 * (c - 3) + s), i1 + 8 * (2 * (c - 3) + s)
            if j <= i1:
                of[c, k] = (i1 + 1) * i1 // 2 + j
    return of


def kernel(**inputs):
    import concourse.bacc as _bacc
    from concourse.bass_utils import run_bass_kernel_spmd as _run

    a = {k: np.asarray(v) for k, v in inputs.items()}
    tables = [a[f"tbl_{f}"] for f in range(NF)]
    starts = np.cumsum([0] + [t.shape[0] for t in tables[:-1]]).astype(np.int32)

    def by_row(x):
        return np.ascontiguousarray(x.reshape(ROUNDS * TILES, 128).T)

    def columns(x, n):
        return x.reshape(n, 128).T

    def k_major(x):
        return np.ascontiguousarray(x.reshape(-1, 128, x.shape[1]).transpose(1, 0, 2))

    small = {
        "gs": columns(a["L0_rec_gs"], 1), "gd": columns(a["L0_rec_gd"], 1), "bd": columns(a["L0_rec_bd"], 1),
        "gl": columns(a["L0_rec_gl"][:USED], USED // 128), "bl": columns(a["L0_rec_bl"][:USED], USED // 128),
        "b1": columns(a["b_top1"], H1 // 128), "b2": columns(a["b_top2"], H2 // 128),
        "w3": columns(a["W_top3"][:, 0], H2 // 128),
        "gsi": np.tile(a["L0_rec_gsi"][None, :], (128, 1)), "bsi": np.tile(a["L0_rec_bsi"][None, :], (128, 1)),
    }
    of = pair_rows()
    wl = np.zeros((128, CHUNKS, MAXD), a["L0_rec_Wl"].dtype)
    for c in range(CHUNKS):
        used = of[c] >= 0
        wl[used, c, :] = a["L0_rec_Wl"].T[of[c][used]]
    ws_t = np.ascontiguousarray(a["L0_rec_Ws"].T)
    arrays = {
        "tbl": np.concatenate(tables, axis=0),
        "ids": by_row(a["ids"]),
        "base": by_row(np.tile(starts, (B, 1))),
        "ident": np.eye(128, dtype=np.float32),
        "vecs": np.concatenate([small[n] for n in VEC], axis=1),
        "bs_row": np.tile(a["L0_rec_bs"][None, :], (NF, 1)),
        "ws_t": np.concatenate([ws_t, ws_t], axis=0),
        "wsi_blocks": wsi_pattern(a["L0_rec_Wsi"]),
        "dense_t": k_major(np.ascontiguousarray(a["r_dense_t"].T)),
        "wd_t": k_major(np.ascontiguousarray(a["L0_rec_Wd"].T)),
        "wl_chunks": wl,
        "w1": k_major(np.concatenate([a["W_top1"][:USED], a["W_top1"][MAXD:]], axis=0)),
        "w2": k_major(a["W_top2"]),
    }
    nc = _bacc.Bacc("TRN2", target_bir_lowering=False, num_devices=1)
    args = []
    for name, x in arrays.items():
        arrays[name] = np.ascontiguousarray(x)
        args.append(nc.dram_tensor(name, x.shape, mybir.dt.from_np(x.dtype), kind="ExternalInput").ap())
    args.append(nc.dram_tensor("out", (1, B), mybir.dt.float32, kind="ExternalOutput").ap())
    dlrm_tower(nc, *args)
    r = _run(nc, [arrays], core_ids=[0])
    return r.results[0]["out"].reshape(B, 1)
```

```python
from contextlib import ExitStack

import numpy as np

import concourse.bass as bass
from concourse import mybir

B = 512
NF = 26
D = 64
E = 128
P = 32
MAXD, USED = 512, 384
DD = 256
H1, H2 = 512, 256
EPS = 1e-5

BT = 128
ROUNDS = B // BT
TILES = BT * NF // 128
STARTS = [0, 4, 8, 10, 14, 18, 20, 24, TILES]
GROUPS = len(STARTS) - 1
GT = 4
BANK_B = 16
BANKS = BT // BANK_B
PATTERN = 13
PATTERN_B = PATTERN * 128 // NF
BLK = 6
CHUNKS = 5
ZB = BT // 4
ZK = 512 // (P + 1)
SUMS = P + 2
TOPK = (USED + DD) // 128

W_LAG = 3
Z_LAG = 5


def group_tiles(q):
    return list(range(STARTS[q], STARTS[q + 1]))


def bank_parts(m):
    mm, base = m % (BANKS // 2), PATTERN * (m // (BANKS // 2))
    parts = []
    for tt in range(BANK_B * NF * mm // 128, (BANK_B * NF * (mm + 1) - 1) // 128 + 1):
        first, last = 128 * tt // NF, (128 * tt + 127) // NF
        lo, hi = max(first, BANK_B * mm), min(last, BANK_B * mm + BANK_B - 1)
        parts.append((base + tt, tt, P * (lo - BANK_B * mm), P * (hi + 1 - BANK_B * mm), lo - first, hi + 1 - first))
    return parts


def last_bank(q):
    return max(m for m in range(BANKS) if any(p[0] in group_tiles(q) for p in bank_parts(m)))


assert all(bank_parts(m)[-1][0] in group_tiles(m) for m in range(BANKS))

VEC = {}
for _name, _n in (("gs", 1), ("gd", 1), ("bd", 1), ("gl", USED // 128), ("bl", USED // 128), ("b1", H1 // 128),
                  ("b2", H2 // 128), ("w3", H2 // 128), ("g_i", CHUNKS), ("g_j", CHUNKS), ("b_i", CHUNKS),
                  ("b_j", CHUNKS)):
    VEC[_name] = (sum(n for _, n in VEC.values()), _n)
NVEC = sum(n for _, n in VEC.values())


def dlrm_tower(nc, tbl, ids, base, ident, vecs, bs_row, ws_t, wsi_rows, places, dense_t, wd_t, wl_chunks, picks, w1, w2, out):
    fp32, i32 = mybir.dt.float32, mybir.dt.int32
    ALU, ACT, AX = mybir.AluOpType, mybir.ActivationFunctionType, mybir.AxisListType

    ctx = ExitStack()
    with ctx:
        def sb(name, shape, dt=fp32):
            return ctx.enter_context(nc.sbuf_tensor(name, shape, dt))

        def ps(name, shape):
            return ctx.enter_context(nc.psum_tensor(name, shape, fp32))

        def sem(name):
            return ctx.enter_context(nc.semaphore(name))

        idx = sb("idx", [128, ROUNDS * TILES], i32)
        idx_base = sb("idx_base", [128, ROUNDS * TILES], i32)
        identity = sb("identity", [128, 128])
        vec = sb("vec", [128, NVEC])
        bs_rep = sb("bs_rep", [NF, E])
        ws_raw = sb("ws_raw", [128, E])
        ws_mean = sb("ws_mean", [128, 1])
        ws_diag = sb("ws_diag", [128, 2, E])
        wsi = sb("wsi", [128, PATTERN, BLK, P])
        wsi_raw = sb("wsi_raw", [128, PATTERN, P])
        wsi_mean = sb("wsi_mean", [128, PATTERN])
        place = sb("place", [128, PATTERN, BLK])
        shift = sb("shift", [128, P])
        dense = sb("dense", [128, DD // 128, B])
        wd = sb("wd", [128, DD // 128, E])
        wl = sb("wl", [128, CHUNKS, MAXD])
        pick = sb("pick", [128, 3, CHUNKS, SUMS])
        gb = sb("gb", [128, 4, CHUNKS])
        sum_mix = sb("sum_mix", [128, CHUNKS, SUMS])
        wl_sum = sb("wl_sum", [SUMS, MAXD])
        w_top1 = sb("w_top1", [128, TOPK, H1])
        w_top2 = sb("w_top2", [128, H1 // 128, H2])
        eps = sb("eps", [128, 1])

        def col(name, k=0, n=1):
            at = VEC[name][0] + k
            return vec[:, at:at + n]

        xn = sb("xn", [128, ROUNDS, E])
        x_stats = sb("x_stats", [128, ROUNDS, 6])
        x_mean_var = sb("x_mean_var", [128, ROUNDS, 2])
        x_std = sb("x_std", [128, ROUNDS])
        x_rstd = sb("x_rstd", [128, ROUNDS])
        x_t = sb("x_t", [128, B])
        emb = sb("emb", [128, TILES, D])
        emb_t = sb("emb_t", [128, 2, 2, 128])
        u_sq = sb("u_sq", [128, 2, GT, E])
        u_var = sb("u_var", [128, 2, GT])
        u_std = sb("u_std", [128, 2, GT])
        u_rstd = sb("u_rstd", [128, 2, GT])
        u_norm = sb("u_norm", [128, TILES, E])
        y = sb("y", [128, 2, BANK_B, P])
        y_sq = sb("y_sq", [128, 2, BANK_B, P])
        y_var = sb("y_var", [128, 2, BANK_B])
        y_std = sb("y_std", [128, 2, BANK_B])
        y_rstd = sb("y_rstd", [128, 2, BANK_B])
        x_sum = sb("x_sum", [128, ROUNDS])
        rows = sb("rows", [128, P + 2, BT])
        z_raw = sb("z_raw", [128, ZB, P + 1])
        z = sb("z", [128, P, P])
        z_pack = sb("z_pack", [128, CHUNKS * 128 + SUMS])
        z_t = sb("z_t", [128, CHUNKS + 1, BT])
        stats = sb("stats", [128, 6])
        mean_var = sb("mean_var", [128, 2])
        carrier = sb("carrier", [128, 10])
        l_std = sb("l_std", [128, 1])
        l_rstd = sb("l_rstd", [128, 1])
        l_norm = sb("l_norm", [128, USED])
        l_t = sb("l_t", [128, USED // 128, BT])
        h1 = sb("h1", [128, H1 // 128, BT])
        h2 = sb("h2", [128, H2 // 128, B])
        y_out = sb("y_out", [1, B])

        ps_u = [ps(f"ps_u{i}", [128, GT, E]) for i in range(2)]
        ps_y = [ps(f"ps_y{i}", [128, BANK_B, P]) for i in range(2)]
        ps_z = ps("ps_z", [128, 3, 512])
        ps_p = ps("ps_p", [128, 512])

        ids_in, base_in, ident_in, vec_in, bs_in = (sem(n) for n in ("ids_in", "base_in", "ident_in", "vec_in", "bs_in"))
        ws_in, wsi_in, dense_in, wd_in = (sem(n) for n in ("ws_in", "wsi_in", "dense_in", "wd_in"))
        wl_in, pick_in, w1_in, w2_in = (sem(n) for n in ("wl_in", "pick_in", "w1_in", "w2_in"))
        gb_ready, mix_step, sum_mm, wl_sum_ready, wl_scaled = (
            sem(n) for n in ("gb_ready", "mix_step", "sum_mm", "wl_sum_ready", "wl_scaled"))
        idx_ready = sem("idx_ready")
        gathered = [sem(f"gathered{q}") for q in range(GROUPS)]
        filled = sem("filled")
        ws_step, wsi_step = sem("ws_step"), sem("wsi_step")
        shift_mm, shift_ready, sx_mm, sx_ready = (sem(n) for n in ("shift_mm", "shift_ready", "sx_mm", "sx_ready"))
        x_mm, x_stat, x_aggr, x_root, x_inv, x_norm, x_tr, x_ready = (
            sem(n) for n in ("x_mm", "x_stat", "x_aggr", "x_root", "x_inv", "x_norm", "x_tr", "x_ready"))
        emb_turned, emb_copied = sem("emb_turned"), sem("emb_copied")
        u_mm, u_squared, u_root, u_inv, u_scaled = (
            sem(n) for n in ("u_mm", "u_squared", "u_root", "u_inv", "u_scaled"))
        y_mm, y_shifted, y_squared, y_summed, y_root, y_inv, y_scaled = (
            sem(n) for n in ("y_mm", "y_shifted", "y_squared", "y_summed", "y_root", "y_inv", "y_scaled"))
        x_placed, z_mm, z_copied, sx_copied, z_ready, z_packed = (
            sem(n) for n in ("x_placed", "z_mm", "z_copied", "sx_copied", "z_ready", "z_packed"))
        z_turned, zt_copied, l_mm, l_stat, l_aggr, l_root, l_inv, l_scaled, l_turned, lt_ready = (
            sem(n) for n in ("z_turned", "zt_copied", "l_mm", "l_stat", "l_aggr", "l_root", "l_inv", "l_scaled",
                             "l_turned", "lt_ready"))
        late_h1_mm, late_h1_ready, late_h2_mm, late_h2_ready = (
            sem(n) for n in ("late_h1_mm", "late_h1_ready", "late_h2_mm", "late_h2_ready"))
        h1_mm, h1_ready, h2_mm, h2_ready, out_mm, out_copied, stored = (
            sem(n) for n in ("h1_mm", "h1_ready", "h2_mm", "h2_ready", "out_mm", "out_copied", "stored"))

        def live(t):
            return not isinstance(t[0], int) or 0 <= t[0] + t[1] < ROUNDS

        def count(per_round, t, n):
            return t[0] * per_round + (t[1] * per_round + n)

        def past(per_round, t, n):
            return count(per_round, t, n + 1)

        def wait(eng, s, n):
            if not isinstance(n, int) or n > 0:
                eng.wait_ge(s, n)

        def in_rounds(t):
            return live((t[0], 0))

        def after(t, n):
            return isinstance(t[0], int) and t[0] == ROUNDS + n - 1

        def first(t):
            return isinstance(t[0], int) and t[0] == 0

        def at(t, q, lag):
            return (t[0], t[1] + (q - lag) // GROUPS), (q - lag) % GROUPS

        def z_cols(bb):
            at = (P + 1) * (bb % ZK)
            return bb // ZK, slice(at, at + P + 1)

        def run(eng, step):
            for r in range(2):
                for q in range(GROUPS):
                    step((r, 0), q)
            with eng.Fori(2, ROUNDS) as t:
                for q in range(GROUPS):
                    step((t, 0), q)
            for r in range(ROUNDS, ROUNDS + 2):
                for q in range(GROUPS):
                    step((r, 0), q)

        LATE = (ROUNDS - 2, ROUNDS - 1)
        LAYER_K, DENSE_K = tuple(range(USED // 128)), tuple(range(USED // 128, TOPK))

        def late_bank(c):
            return ps_u[c][:, 0, :] if c < 2 else ps_y[c - 2][:, 0:BT // P, :].rearrange("p a b -> p (a b)")

        block = ctx.enter_context(nc.Block())

        @block.sync
        def _(sp):
            sp.dma_start(idx[:, :], ids).then_inc(ids_in, 16)
            sp.dma_start(idx_base[:, :], base).then_inc(base_in, 16)
            sp.dma_start(ws_raw[:, :], ws_t).then_inc(ws_in, 16)
            sp.dma_start(wsi_raw[:, :, :], wsi_rows).then_inc(wsi_in, 16)
            sp.dma_start(place[:, :, :], places).then_inc(wsi_in, 16)
            sp.dma_start(identity[:, :], ident).then_inc(ident_in, 16)
            sp.dma_start(wd[:, :, :], wd_t).then_inc(wd_in, 16)
            sp.dma_start(dense[:, :, :], dense_t).then_inc(dense_in, 16)
            sp.dma_start(vec[:, :], vecs).then_inc(vec_in, 16)
            sp.dma_start(bs_rep[:, :], bs_row).then_inc(bs_in, 16)
            sp.wait_ge(gathered[0], 16 * len(group_tiles(0)))
            sp.dma_start(pick[:, :, :, :], picks).then_inc(pick_in, 16)
            sp.wait_ge(gathered[2], 16 * len(group_tiles(2)))
            sp.dma_start(wl[:, :, :], wl_chunks).then_inc(wl_in, 16)
            sp.wait_ge(gathered[4], 16 * len(group_tiles(4)))
            sp.dma_start(w_top1[:, :, :], w1).then_inc(w1_in, 16)
            sp.wait_ge(gathered[6], 16 * len(group_tiles(6)))
            sp.dma_start(w_top2[:, :, :], w2).then_inc(w2_in, 16)
            sp.wait_ge(out_copied, 2)
            sp.dma_start(out, y_out[:, :]).then_inc(stored, 16)
            sp.wait_ge(stored, 16)

        @block.gpsimd
        def _(pool):
            pool.wait_ge(idx_ready, 1)
            for t in range(ROUNDS):
                for q in range(GROUPS):
                    wait(pool, emb_turned, GROUPS * (t - 1) + q + 1)
                    for k in group_tiles(q):
                        g = TILES * t + k
                        pool.indirect_dma_start(
                            emb[:, k, :], None, tbl, bass.IndirectOffsetOnAxis(ap=idx[:, g:g + 1], axis=0),
                        ).then_inc(gathered[q], 16)

        @block.tensor
        def _(pe):
            def project_dense(rounds):
                pe.wait_ge(dense_in, 16)
                pe.wait_ge(wd_in, 16)
                for r in rounds:
                    for k in range(DD // 128):
                        mm = nc.tensor.matmul(ps_p[:, E * r:E * (r + 1)], dense[:, k, BT * r:BT * (r + 1)], wd[:, k, :],
                                              start=(k == 0), stop=(k == DD // 128 - 1))
                if rounds[-1] == ROUNDS - 1:
                    mm.then_inc(x_mm, 1)

            def turn_dense():
                pe.wait_ge(x_norm, 1)
                for r in range(ROUNDS):
                    mm = nc.tensor.transpose(ps_p[:, BT * r:BT * (r + 1)], xn[:, r, :], identity[:, :])
                mm.then_inc(x_tr, 1)

            def bias_rows():
                pe.wait_ge(x_ready, 1)
                pe.wait_ge(bs_in, 16)
                pe.wait_ge(wsi_step, 3)
                pe.wait_ge(filled, 4)
                nc.tensor.matmul(ps_p[:, 0:P], bs_rep[:, :], wsi[0:NF, 0, 0, :], start=True, stop=True)
                for r in range(ROUNDS):
                    mm = nc.tensor.matmul(ps_p[:, P + r:P + r + 1], x_t[:, BT * r:BT * (r + 1)], rows[:, 0, 0:1],
                                          start=True, stop=True)
                mm.then_inc(shift_mm, 1)

            def weights_of_sums(chunks):
                if chunks[0] == 0:
                    pe.wait_ge(sx_ready, 1)
                    pe.wait_ge(wl_in, 16)
                    pe.wait_ge(mix_step, 3 * CHUNKS)
                for c in chunks:
                    nc.tensor.matmul(ps_p[0:SUMS, :], sum_mix[:, c, :], wl[:, c, :], start=(c == 0),
                                     stop=(c == CHUNKS - 1)).then_inc(sum_mm, 1)

            def turn_gathers(t, q):
                pe.wait_ge(gathered[q], count(16 * len(group_tiles(q)), t, 16 * len(group_tiles(q))))
                wait(pe, u_scaled, count(GROUPS, t, q - 1))
                for i, k in enumerate(group_tiles(q)[::2]):
                    mm = nc.tensor.transpose(ps_u[q % 2][:, i, :],
                                             emb[:, k:k + 2, :].rearrange("p k d -> p (k d)"), identity[:, :])
                mm.then_inc(emb_turned, 1)

            def project(t, q):
                pe.wait_ge(emb_copied, count(GROUPS, t, q + 1))
                for i in range(len(group_tiles(q)) // 2):
                    mm = nc.tensor.matmul(ps_u[q % 2][:, 2 * i:2 * i + 2, :], emb_t[:, q % 2, i, :], ws_diag[:, :, :],
                                          start=True, stop=True)
                mm.then_inc(u_mm, 1)

            def mix_features(t, m):
                pe.wait_ge(u_scaled, count(GROUPS, t, m + 1))
                wait(pe, y_shifted, count(BANKS, t, m - 1))
                parts = bank_parts(m)
                flat = ps_y[m % 2][:, :, :].rearrange("p b r -> p (b r)")
                for n, (tile, tt, lo, hi, b0, b1) in enumerate(parts):
                    mm = nc.tensor.matmul(flat[:, lo:hi], u_norm[:, tile, :], wsi[:, tt, b0:b1, :],
                                          start=(n == 0), stop=(n == len(parts) - 1), skip_group_check=True)
                mm.then_inc(y_mm, 1)

            def pairs(t, m):
                pe.wait_ge(y_scaled, count(BANKS, t, m + 1))
                if m == 0:
                    pe.wait_ge(x_placed, count(1, t, 1))
                    wait(pe, z_copied, count(1, t, 0))
                for b in range(BANK_B * m, BANK_B * (m + 1)):
                    quarter, bb = b // 32, b % 32
                    bank, cols = z_cols(bb)
                    mm = nc.tensor.matmul(ps_z[32 * quarter:32 * quarter + 32, bank, cols], rows[:, 2:P + 2, b],
                                          rows[:, 0:P + 1, b], start=True, stop=True)
                mm.then_inc(z_mm, 1)

            def turn_pairs(t, chunks):
                if chunks[0] == 0:
                    pe.wait_ge(sx_copied, count(1, t, 1))
                    if in_rounds(t):
                        wait(pe, h2_ready, count(1, t, 0))
                    else:
                        pe.wait_ge(lt_ready, LATE[1])
                    pe.wait_ge(z_packed, past(1, t, 1))
                else:
                    pe.wait_ge(zt_copied, count(2, t, 1))
                for i, c in enumerate(chunks):
                    k = 128 if c < CHUNKS else SUMS
                    mm = nc.tensor.transpose(ps_p[0:k, BT * i:BT * (i + 1)], z_pack[:, 128 * c:128 * c + k], identity[:, :])
                mm.then_inc(z_turned, 1)

            def interaction_layer(t, chunks):
                if chunks[0] == 0:
                    pe.wait_ge(zt_copied, count(2, t, 2))
                    pe.wait_ge(wl_sum_ready, 1)
                    pe.wait_ge(wl_scaled, 1)
                for c in chunks:
                    k = 128 if c < CHUNKS else SUMS
                    mm = nc.tensor.matmul(ps_p[:, :], z_t[0:k, c, :], wl[:, c, :] if c < CHUNKS else wl_sum[:, :],
                                          start=(c == 0), stop=(c == CHUNKS))
                if chunks[-1] == CHUNKS:
                    mm.then_inc(l_mm, 1)

            def turn_layer(t):
                pe.wait_ge(l_scaled, count(1, t, 1))
                for c in range(USED // 128):
                    mm = nc.tensor.transpose(ps_p[:, BT * c:BT * (c + 1)], l_norm[:, 128 * c:128 * (c + 1)], identity[:, :])
                mm.then_inc(l_turned, 1)

            def top1(t, chunks):
                if chunks[0] == 0:
                    pe.wait_ge(w1_in, 16)
                    pe.wait_ge(lt_ready, count(1, t, 1))
                for c in chunks:
                    for k in range(TOPK):
                        kd = k - USED // 128
                        mm = nc.tensor.matmul(ps_p[:, BT * c:BT * (c + 1)], w_top1[:, k, 128 * c:128 * (c + 1)],
                                              l_t[:, k, :] if kd < 0 else dense[:, kd, bass.ds((t[0] + t[1]) * BT, BT)],
                                              start=(k == 0), stop=(k == TOPK - 1))
                mm.then_inc(h1_mm, 1)

            def top2(t):
                pe.wait_ge(w2_in, 16)
                pe.wait_ge(h1_ready, count(1, t, 1))
                for c in range(H2 // 128):
                    for k in range(H1 // 128):
                        mm = nc.tensor.matmul(ps_p[:, BT * c:BT * (c + 1)], w_top2[:, k, 128 * c:128 * (c + 1)],
                                              h1[:, k, :], start=(k == 0), stop=(k == H1 // 128 - 1))
                mm.then_inc(h2_mm, 1)

            def late_top1(late, ks, chunks=range(H1 // 128)):
                r = LATE[late]
                if ks[0] == DENSE_K[0]:
                    pe.wait_ge(u_scaled, GROUPS * ROUNDS)
                    if chunks[-1] >= 2:
                        pe.wait_ge(y_shifted, BANKS * ROUNDS)
                    wait(pe, late_h1_ready, 4 * late)
                if ks[-1] == LAYER_K[-1]:
                    pe.wait_ge(lt_ready, r + 1)
                for c in chunks:
                    for k in ks:
                        kd = k - USED // 128
                        mm = nc.tensor.matmul(late_bank(c), w_top1[:, k, 128 * c:128 * (c + 1)],
                                              l_t[:, k, :] if kd < 0 else dense[:, kd, BT * r:BT * (r + 1)],
                                              start=(k == DENSE_K[0]), stop=(k == LAYER_K[-1]))
                    if ks[-1] == LAYER_K[-1]:
                        mm.then_inc(late_h1_mm, 1)

            def late_top2(late):
                if late == 0:
                    pe.wait_ge(z_copied, ROUNDS)
                else:
                    pe.wait_ge(late_h2_ready, 1)
                for k in range(H1 // 128):
                    pe.wait_ge(late_h1_ready, H1 // 128 * late + k + 1)
                    for c in range(H2 // 128):
                        mm = nc.tensor.matmul(ps_z[:, c, 0:BT], w_top2[:, k, 128 * c:128 * (c + 1)], h1[:, k, :],
                                              start=(k == 0), stop=(k == H1 // 128 - 1))
                mm.then_inc(late_h2_mm, 1)

            def output(b0, b1):
                for k in range(H2 // 128):
                    mm = nc.tensor.matmul(ps_z[0:1, 2, b0:b1], col("w3", k), h2[:, k, b0:b1],
                                          start=(k == 0), stop=(k == H2 // 128 - 1))
                mm.then_inc(out_mm, 1)

            def early_top3():
                pe.wait_ge(h2_ready, LATE[0])
                pe.wait_ge(late_h2_ready, 1)
                output(0, BT * LATE[1])

            def top3():
                pe.wait_ge(late_h2_ready, 2)
                pe.wait_ge(out_copied, 1)
                output(BT * LATE[1], B)

            def step(t, q):
                before, older = (t[0], t[1] - 1), (t[0], t[1] - 2)
                tl, ql = at(t, q, 1)
                if live(tl):
                    project(tl, ql)
                if live(older) and q == 0:
                    interaction_layer(older, (3,))
                tl, ql = at(t, q, W_LAG)
                if live(tl):
                    mix_features(tl, ql)
                if live(before):
                    if q == 6:
                        turn_pairs(before, (0, 1, 2, 3))
                    if q == 7:
                        interaction_layer(before, (0, 1))
                if live(older) and q == 0:
                    interaction_layer(older, (4,))
                if live(t):
                    turn_gathers(t, q)
                if after(t, 1) and q in (3, 4):
                    late_top1(0, DENSE_K + LAYER_K, (q - 3,))
                tl, ql = at(t, q, Z_LAG)
                if live(tl):
                    pairs(tl, ql)
                if live(before):
                    if q == 6 and in_rounds(t):
                        turn_pairs(before, (4, 5))
                    if q == 7:
                        interaction_layer(before, (2,))
                if after(t, 1):
                    if q == 4:
                        late_top1(0, DENSE_K + LAYER_K, (2, 3))
                    if q == 6:
                        late_top2(0)
                        turn_pairs(before, (4, 5))
                    if q == 7:
                        early_top3()
                if live(older):
                    if q == 0:
                        interaction_layer(older, (5,))
                    if q == 1:
                        if not live(before):
                            late_top1(1, DENSE_K)
                        turn_layer(older)
                    if q == 2 and in_rounds(t):
                        top1(older, (0, 1))
                    if q == 3 and in_rounds(t):
                        top1(older, (2, 3))
                    if q == 4 and in_rounds(t):
                        top2(older)
                if first(t):
                    if q == 0:
                        project_dense((2, 3))
                    if q == 1:
                        turn_dense()
                    if q == 2:
                        bias_rows()
                    if q == 4:
                        weights_of_sums((0, 1))
                    if q == 5:
                        weights_of_sums((2, 3))
                    if q == 6:
                        weights_of_sums((4,))

            pe.wait_ge(ident_in, 16)
            pe.wait_ge(ws_step, 3)
            project_dense((0, 1))
            run(pe, step)
            pe.wait_ge(vec_in, 16)
            late_top1(1, LAYER_K)
            late_top2(1)
            top3()

        @block.scalar
        def _(act):
            act.wait_ge(filled, 1)
            nc.scalar.activation(l_std[:, :], eps[:, :], ACT.Sqrt)

            def root_dense():
                act.wait_ge(x_aggr, ROUNDS)
                nc.scalar.activation(x_std[:, :], x_mean_var[:, :, 1], ACT.Sqrt, bias=eps[:, :]).then_inc(x_root, 1)

            def scale_dense():
                act.wait_ge(vec_in, 16)
                act.wait_ge(x_tr, 1)
                nc.scalar.activation(x_t[:, :], ps_p[:, :], ACT.Identity, bias=col("bd"), scale=col("gd")).then_inc(x_ready, 1)

            def copy_bias_rows():
                act.wait_ge(shift_mm, 1)
                nc.scalar.copy(shift[:, :], ps_p[:, 0:P]).then_inc(shift_ready, 1)
                nc.scalar.copy(x_sum[:, :], ps_p[:, P:P + ROUNDS]).then_inc(sx_ready, 1)

            def copy_weights_of_sums():
                act.wait_ge(sum_mm, CHUNKS)
                nc.scalar.copy(wl_sum[:, :], ps_p[0:SUMS, :]).then_inc(wl_sum_ready, 1)

            def copy_gathers(t, q):
                n = len(group_tiles(q)) // 2
                act.wait_ge(emb_turned, count(GROUPS, t, q + 1))
                wait(act, u_mm, count(GROUPS, t, q - 1))
                nc.scalar.copy(emb_t[:, q % 2, 0:n, :], ps_u[q % 2][:, 0:n, :]).then_inc(emb_copied, 1)

            def square_u(t, q):
                n = len(group_tiles(q))
                act.wait_ge(u_mm, count(GROUPS, t, q + 1))
                for k in range(n):
                    a = nc.scalar.activation(u_sq[:, q % 2, k, :], ps_u[q % 2][:, k, :], ACT.Square,
                                             accum_out=u_var[:, q % 2, k:k + 1])
                a.then_inc(u_squared, 1)

            def root_u(t, q):
                n = len(group_tiles(q))
                act.wait_ge(u_squared, count(GROUPS, t, q + 1))
                wait(act, u_inv, count(GROUPS, t, q - 1))
                nc.scalar.activation(u_std[:, q % 2, 0:n], u_var[:, q % 2, 0:n], ACT.Sqrt, bias=eps[:, :],
                                     scale=1.0 / E).then_inc(u_root, 1)

            def square_y(t, m):
                act.wait_ge(y_shifted, count(BANKS, t, m + 1))
                wait(act, y_summed, count(BANKS, t, m - 1))
                nc.scalar.activation(y_sq[:, m % 2, :, :], y[:, m % 2, :, :], ACT.Square).then_inc(y_squared, 1)

            def root_y(t, m):
                act.wait_ge(y_summed, count(BANKS, t, m + 1))
                wait(act, y_inv, count(BANKS, t, m - 1))
                nc.scalar.activation(y_std[:, m % 2, :], y_var[:, m % 2, :], ACT.Sqrt, bias=eps[:, :],
                                     scale=1.0 / P).then_inc(y_root, 1)

            def place_x(t):
                wait(act, z_mm, past(BANKS, t, 0))
                nc.scalar.copy(rows[:, 1, :], x_t[:, bass.ds((t[0] + t[1]) * BT, BT)]).then_inc(x_placed, 1)

            def copy_z(t):
                act.wait_ge(z_mm, past(BANKS, t, BANKS))
                wait(act, z_ready, past(1, t, 0))
                for first in range(0, ZB, ZK):
                    n = min(ZK, ZB - first)
                    a = nc.scalar.copy(z_raw[:, first:first + n, :], ps_z[:, first // ZK, 0:n * (P + 1)].rearrange(
                        "p (b j) -> p b j", b=n))
                a.then_inc(z_copied, 1)
                wait(act, z_turned, past(2, t, 0))
                nc.scalar.copy(z_pack[:, CHUNKS * 128 + P:CHUNKS * 128 + P + 1], x_sum[:, bass.ds(t[0] + t[1], 1)]).then_inc(sx_copied, 1)

            def copy_pairs(t, n):
                act.wait_ge(z_turned, past(2, t, n + 1))
                wait(act, l_mm, past(1, t, 0))
                if n == 0:
                    nc.scalar.copy(z_t[:, 0:4, :], ps_p[:, :].rearrange("p (k b) -> p k b", k=4)).then_inc(zt_copied, 1)
                else:
                    nc.scalar.copy(z_t[:, 4, :], ps_p[:, 0:BT])
                    nc.scalar.copy(z_t[0:SUMS, 5, :], ps_p[0:SUMS, BT:2 * BT]).then_inc(zt_copied, 1)

            def root_l(t):
                act.wait_ge(l_aggr, count(1, t, 1))
                nc.scalar.activation(l_std[:, :], mean_var[:, 1:2], ACT.Sqrt, bias=eps[:, :]).then_inc(l_root, 1)

            def scale_l(t):
                act.wait_ge(l_turned, count(1, t, 1))
                if after(t, 2):
                    act.wait_ge(late_h1_mm, H1 // 128)
                else:
                    wait(act, h1_mm, past(2, t, 0))
                for c in range(USED // 128):
                    a = nc.scalar.activation(l_t[:, c, :], ps_p[:, BT * c:BT * (c + 1)], ACT.Identity, bias=col("bl", c),
                                             scale=col("gl", c))
                a.then_inc(lt_ready, 1)

            def relu1(t):
                act.wait_ge(h1_mm, past(2, t, 2))
                wait(act, h2_mm, past(1, t, 0))
                for c in range(H1 // 128):
                    a = nc.scalar.activation(h1[:, c, :], ps_p[:, BT * c:BT * (c + 1)], ACT.Relu, bias=col("b1", c))
                a.then_inc(h1_ready, 1)

            def relu2(t):
                act.wait_ge(h2_mm, past(1, t, 1))
                for c in range(H2 // 128):
                    a = nc.scalar.activation(h2[:, c, bass.ds((t[0] + t[1]) * BT, BT)], ps_p[:, BT * c:BT * (c + 1)],
                                             ACT.Relu, bias=col("b2", c))
                a.then_inc(h2_ready, 1)

            def relu1_late(late):
                if late == 0:
                    act.wait_ge(h2_mm, 1 + LATE[0])
                else:
                    act.wait_ge(late_h2_mm, 1)
                for c in range(H1 // 128):
                    act.wait_ge(late_h1_mm, H1 // 128 * late + c + 1)
                    nc.scalar.activation(h1[:, c, :], late_bank(c), ACT.Relu, bias=col("b1", c)).then_inc(late_h1_ready, 1)

            def relu2_late(late):
                r = LATE[late]
                act.wait_ge(late_h2_mm, late + 1)
                for c in range(H2 // 128):
                    a = nc.scalar.activation(h2[:, c, BT * r:BT * (r + 1)], ps_z[:, c, 0:BT], ACT.Relu, bias=col("b2", c))
                a.then_inc(late_h2_ready, 1)

            def step(t, q):
                before, older = (t[0], t[1] - 1), (t[0], t[1] - 2)
                if live(before):
                    if q == 5:
                        copy_z(before)
                    if q == 7:
                        copy_pairs(before, 1)
                if live(t) and q == 5:
                    place_x(t)
                if live(older):
                    if q == 1:
                        root_l(older)
                    if q == 4 and in_rounds(t):
                        relu1(older)
                tl, ql = at(t, q, 1)
                if live(tl):
                    square_u(tl, ql)
                    root_u(tl, ql)
                ty, qy = at(t, q, W_LAG + 1)
                if live(ty):
                    root_y(ty, qy)
                if live(before) and q == 6:
                    copy_pairs(before, 0)
                if live(t):
                    copy_gathers(t, q)
                if live(older) and q == 5 and in_rounds(t):
                    relu2(older)
                tl, ql = at(t, q, W_LAG)
                if live(tl):
                    square_y(tl, ql)
                if live(older) and q == 1:
                    scale_l(older)
                if after(t, 2) and q == 0:
                    act.wait_ge(out_mm, 1)
                    nc.scalar.copy(y_out[:, 0:BT * LATE[1]], ps_z[0:1, 2, 0:BT * LATE[1]]).then_inc(out_copied, 1)
                if after(t, 1):
                    if q == 5:
                        relu1_late(0)
                    if q == 7:
                        relu2_late(0)
                if first(t):
                    if q == 0:
                        root_dense()
                    if q == 1:
                        scale_dense()
                    if q == 2:
                        copy_bias_rows()
                    if q == 6:
                        copy_weights_of_sums()

            run(act, step)
            relu1_late(1)
            relu2_late(1)
            act.wait_ge(out_mm, 2)
            nc.scalar.copy(y_out[:, BT * LATE[1]:], ps_z[0:1, 2, BT * LATE[1]:]).then_inc(out_copied, 1)

        @block.vector
        def _(dve):
            nc.vector.memset(eps[:, :], EPS).then_inc(filled, 1)
            nc.vector.memset(ws_diag[:, :, :], 0.0).then_inc(filled, 1)
            nc.vector.memset(rows[:, 0, :], 1.0).then_inc(filled, 1)
            nc.vector.memset(z_pack[:, CHUNKS * 128 + P + 1:], 1.0).then_inc(filled, 1)
            for n, s in enumerate((y_mm, z_mm, z_ready, z_packed, z_turned, l_mm, h1_mm, h2_mm)):
                nc.vector.memset(carrier[:, 1 + n:2 + n], 0.0).then_inc(s, 1)
            dve.wait_ge(ids_in, 16)
            dve.wait_ge(base_in, 16)
            nc.vector.tensor_tensor(idx[:, :], idx[:, :], idx_base[:, :], ALU.add).then_inc(idx_ready, 1)
            dve.wait_ge(ws_in, 16)
            nc.vector.tensor_reduce(ws_mean[:, :], ws_raw[:, :], AX.X, ALU.add).then_inc(ws_step, 1)
            dve.wait_ge(ws_step, 1)
            nc.vector.tensor_scalar(ws_mean[:, :], ws_mean[:, :], 1.0 / E, None, ALU.mult).then_inc(ws_step, 1)
            dve.wait_ge(ws_step, 2)
            dve.wait_ge(filled, 2)
            for half in range(2):
                rows_of = slice(D * half, D * (half + 1))
                c = nc.vector.tensor_scalar(ws_diag[rows_of, half, :], ws_raw[rows_of, :], ws_mean[rows_of, :], None,
                                            ALU.subtract)
            c.then_inc(ws_step, 1)
            def place_wsi():
                dve.wait_ge(wsi_in, 32)
                nc.vector.tensor_reduce(wsi_mean[:, :], wsi_raw[:, :, :], AX.X, ALU.add).then_inc(wsi_step, 1)
                dve.wait_ge(wsi_step, 1)
                nc.vector.scalar_tensor_tensor(wsi_raw[:, :, :], wsi_mean[:, :].unsqueeze(2).broadcast_to([128, PATTERN, P]),
                                               -1.0 / P, wsi_raw[:, :, :], ALU.mult, ALU.add).then_inc(wsi_step, 1)
                dve.wait_ge(wsi_step, 2)
                for b in range(BLK):
                    a = nc.vector.tensor_tensor(wsi[:, :, b, :], wsi_raw[:, :, :],
                                                place[:, :, b:b + 1].broadcast_to([128, PATTERN, P]), ALU.mult)
                a.then_inc(wsi_step, 1)

            def norm_dense():
                dve.wait_ge(x_mm, 1)
                for r in range(ROUNDS):
                    nc.vector.bn_stats(x_stats[:, r, :], ps_p[:, E * r:E * (r + 1)]).then_inc(x_stat, 1)
                for r in range(ROUNDS):
                    dve.wait_ge(x_stat, r + 1)
                    nc.vector.bn_aggr(x_mean_var[:, r, :], x_stats[:, r, :]).then_inc(x_aggr, 1)

            def scale_dense():
                dve.wait_ge(x_root, 1)
                nc.vector.reciprocal(x_rstd[:, :], x_std[:, :]).then_inc(x_inv, 1)
                dve.wait_ge(x_inv, 1)
                for r in range(ROUNDS):
                    a = nc.vector.tensor_scalar(xn[:, r, :], ps_p[:, E * r:E * (r + 1)], x_mean_var[:, r, 0:1],
                                                x_rstd[:, r:r + 1], ALU.subtract, ALU.mult)
                a.then_inc(x_norm, 1)

            def mix_gsi_bsi():
                dve.wait_ge(vec_in, 16)
                dve.wait_ge(pick_in, 16)
                for n, (a, b) in enumerate((("g_i", "b_j"), ("g_j", "b_i"), ("b_i", "b_j"), ("g_i", "g_j"))):
                    nc.vector.scalar_tensor_tensor(gb[:, n, :], col(a, 0, CHUNKS), float(E) if n == 2 else 1.0,
                                                   col(b, 0, CHUNKS), ALU.mult, ALU.mult).then_inc(gb_ready, 1)
                dve.wait_ge(gb_ready, 4)
                for c in range(CHUNKS):
                    nc.vector.tensor_scalar(sum_mix[:, c, :], pick[:, 0, c, :], gb[:, 0, c:c + 1], None,
                                            ALU.mult).then_inc(mix_step, 1)
                for n in (1, 2):
                    dve.wait_ge(mix_step, n * CHUNKS)
                    for c in range(CHUNKS):
                        nc.vector.scalar_tensor_tensor(sum_mix[:, c, :], pick[:, n, c, :], gb[:, n, c:c + 1],
                                                       sum_mix[:, c, :], ALU.mult, ALU.add).then_inc(mix_step, 1)

            def scale_wl(chunks):
                dve.wait_ge(sum_mm, chunks[-1] + 1)
                for c in chunks:
                    a = nc.vector.tensor_scalar(wl[:, c, :], wl[:, c, :], gb[:, 3, c:c + 1], None, ALU.mult)
                if chunks[-1] == CHUNKS - 1:
                    a.then_inc(wl_scaled, 1)

            def invert_u(t, q):
                n = len(group_tiles(q))
                dve.wait_ge(u_root, count(GROUPS, t, q + 1))
                nc.vector.reciprocal(u_rstd[:, q % 2, 0:n], u_std[:, q % 2, 0:n]).then_inc(u_inv, 1)

            def scale_u(t, q):
                n, k = len(group_tiles(q)), STARTS[q]
                dve.wait_ge(u_inv, count(GROUPS, t, q + 1))
                wait(dve, y_mm, past(BANKS, t, last_bank(q) + 1 - BANKS))
                nc.vector.tensor_tensor(u_norm[:, k:k + n, :], ps_u[q % 2][:, 0:n, :],
                                        u_rstd[:, q % 2, 0:n].unsqueeze(2).broadcast_to([128, n, E]), ALU.mult).then_inc(u_scaled, 1)

            def shift_y(t, m):
                dve.wait_ge(y_mm, past(BANKS, t, m + 1))
                wait(dve, y_scaled, count(BANKS, t, m - 1))
                nc.vector.scalar_tensor_tensor(y[:, m % 2, :, :], ps_y[m % 2][:, :, :], col("gs"),
                                               shift[:, :].unsqueeze(1).broadcast_to([128, BANK_B, P]),
                                               ALU.mult, ALU.add).then_inc(y_shifted, 1)

            def sum_y(t, m):
                dve.wait_ge(y_squared, count(BANKS, t, m + 1))
                wait(dve, y_root, count(BANKS, t, m - 1))
                nc.vector.tensor_reduce(y_var[:, m % 2, :], y_sq[:, m % 2, :, :], AX.X, ALU.add).then_inc(y_summed, 1)

            def invert_y(t, m):
                dve.wait_ge(y_root, count(BANKS, t, m + 1))
                nc.vector.reciprocal(y_rstd[:, m % 2, :], y_std[:, m % 2, :]).then_inc(y_inv, 1)

            def scale_y(t, m):
                b0 = BANK_B * m
                dve.wait_ge(y_inv, count(BANKS, t, m + 1))
                wait(dve, z_mm, past(BANKS, t, m + 1 - BANKS))
                nc.vector.tensor_tensor(rows[:, 2:P + 2, b0:b0 + BANK_B].rearrange("e r b -> e b r"),
                                        y[:, m % 2, :, :], y_rstd[:, m % 2, :].unsqueeze(2).broadcast_to([128, BANK_B, P]),
                                        ALU.mult).then_inc(y_scaled, 1)

            def turn_z(t):
                dve.wait_ge(z_copied, count(1, t, 1))
                wait(dve, z_packed, past(1, t, 0))
                nc.vector.transpose(z[:, :, :], z_raw[:, :, 1:P + 1].rearrange("p b j -> p j b"))
                wait(dve, z_turned, past(2, t, 0))
                nc.vector.transpose(z_pack[:, CHUNKS * 128:CHUNKS * 128 + P], z_raw[:, :, 0]).then_inc(z_ready, 1)
                dve.wait_ge(z_ready, past(1, t, 1))

                def squares(first, step, n):
                    s = z[:, :, :]
                    return bass.AP(s.tensor, s.offset + first, [list(s.ap[0]), [step, n], [P, 8], [1, 8]])

                def packed(c, n):
                    return z_pack[:, 128 * c:128 * (c + n)].rearrange("b (s j i) -> b s j i", j=8, i=8)

                nc.vector.tensor_copy(z_pack[:, 0:256].rearrange("b (j i) -> b j i", j=16), z[:, 0:16, 16:32])
                nc.vector.tensor_copy(packed(2, 1), squares(8, 16 * P + 16, 2))
                nc.vector.tensor_copy(packed(3, 2), squares(0, 8 * P + 8, 4)).then_inc(z_packed, 1)

            def norm_l(t):
                dve.wait_ge(l_mm, past(1, t, 1))
                nc.vector.bn_stats(stats[:, :], ps_p[:, :]).then_inc(l_stat, 1)
                dve.wait_ge(l_stat, count(1, t, 1))
                nc.vector.memset(carrier[:, 0:1], 0.0)
                nc.vector.bn_aggr(mean_var[:, :], stats[:, :]).then_inc(l_aggr, 1)
                dve.wait_ge(l_root, count(1, t, 1))
                nc.vector.reciprocal(l_rstd[:, :], l_std[:, :]).then_inc(l_inv, 1)
                dve.wait_ge(l_inv, count(1, t, 1))
                nc.vector.tensor_scalar(l_norm[:, :], ps_p[:, 0:USED], mean_var[:, 0:1], l_rstd[:, :], ALU.subtract,
                                        ALU.mult).then_inc(l_scaled, 1)

            def step(t, q):
                before, older = (t[0], t[1] - 1), (t[0], t[1] - 2)
                tl, ql = at(t, q, 1)
                tm, qm = at(t, q, W_LAG)
                ty, qy = at(t, q, W_LAG + 1)
                if live(older) and q == 1:
                    norm_l(older)
                if live(before) and q == 5:
                    turn_z(before)
                if live(tm):
                    shift_y(tm, qm)
                if live(tl):
                    invert_u(tl, ql)
                if live(ty):
                    invert_y(ty, qy)
                if live(tl):
                    scale_u(tl, ql)
                if live(ty):
                    scale_y(ty, qy)
                if live(tm):
                    sum_y(tm, qm)
                if first(t):
                    if q == 0:
                        norm_dense()
                        scale_dense()
                    if q == 2:
                        dve.wait_ge(shift_ready, 1)
                    if q == 1:
                        mix_gsi_bsi()
                    if q == 5:
                        scale_wl((0, 1))
                    if q == 6:
                        scale_wl((2, 3))
                    if q == 7:
                        scale_wl((4,))

            place_wsi()
            run(dve, step)


def rows_of_wsi(wsi):
    return np.ascontiguousarray(wsi.T[np.arange(128 * PATTERN) % NF].reshape(PATTERN, 128, P).transpose(1, 0, 2))


def sample_places():
    out = np.zeros((128, PATTERN, BLK), np.float32)
    for tt in range(PATTERN):
        for r in range(128):
            out[r, tt, (128 * tt + r) // NF - 128 * tt // NF] = 1
    return out


def pair_rows():
    of = np.full((CHUNKS, 128, 3), -1)
    for c in range(CHUNKS):
        for k in range(128):
            if c < 2:
                j, i1 = 8 * c + k // 16, 16 + k % 16
            else:
                s, j, i1 = k // 64, k // 8 % 8, k % 8
                if c == 2:
                    j, i1 = j + 16 * s, i1 + 8 + 16 * s
                else:
                    j, i1 = j + 8 * (2 * (c - 3) + s), i1 + 8 * (2 * (c - 3) + s)
            if j <= i1:
                of[c, k] = i1 + 1, j, (i1 + 1) * i1 // 2 + j
    return of


def kernel(**inputs):
    import concourse.bacc as _bacc
    from concourse.bass_utils import run_bass_kernel_spmd as _run

    a = {k: np.asarray(v) for k, v in inputs.items()}
    tables = [a[f"tbl_{f}"] for f in range(NF)]
    starts = np.cumsum([0] + [t.shape[0] for t in tables[:-1]]).astype(np.int32)

    def by_row(x):
        return np.ascontiguousarray(x.reshape(ROUNDS * TILES, 128).T)

    def columns(x, n):
        return x.reshape(n, 128).T

    def k_major(x):
        return np.ascontiguousarray(x.reshape(-1, 128, x.shape[1]).transpose(1, 0, 2))

    small = {
        "gs": columns(a["L0_rec_gs"], 1), "gd": columns(a["L0_rec_gd"], 1), "bd": columns(a["L0_rec_bd"], 1),
        "gl": columns(a["L0_rec_gl"][:USED], USED // 128), "bl": columns(a["L0_rec_bl"][:USED], USED // 128),
        "b1": columns(a["b_top1"], H1 // 128), "b2": columns(a["b_top2"], H2 // 128),
        "w3": columns(a["W_top3"][:, 0], H2 // 128),
    }
    of = pair_rows()
    picks = np.zeros((128, 3, CHUNKS, SUMS), np.float32)
    for name, first, own in (("g", a["L0_rec_gsi"], 1), ("b", a["L0_rec_bsi"], 0)):
        with_row0 = np.concatenate([np.full(1, own, first.dtype), first])
        for side in (0, 1):
            small[f"{name}_{'ij'[side]}"] = np.where(of[:, :, side] >= 0, with_row0[of[:, :, side]], 0).astype(first.dtype).T
    wl = np.zeros((128, CHUNKS, MAXD), a["L0_rec_Wl"].dtype)
    for c in range(CHUNKS):
        used = np.flatnonzero(of[c, :, 2] >= 0)
        wl[used, c, :] = a["L0_rec_Wl"].T[of[c, used, 2]]
        picks[used, 0, c, (of[c, used, 0] - 1) % (P + 1)] = 1
        picks[used, 1, c, (of[c, used, 1] - 1) % (P + 1)] = 1
        picks[used, 2, c, SUMS - 1] = 1
    ws_t = np.ascontiguousarray(a["L0_rec_Ws"].T)
    arrays = {
        "tbl": np.concatenate(tables, axis=0),
        "ids": by_row(a["ids"]),
        "base": by_row(np.tile(starts, (B, 1))),
        "ident": np.eye(128, dtype=np.float32),
        "vecs": np.concatenate([small[n] for n in VEC], axis=1),
        "bs_row": np.tile(a["L0_rec_bs"][None, :], (NF, 1)),
        "ws_t": np.concatenate([ws_t, ws_t], axis=0),
        "wsi_rows": rows_of_wsi(a["L0_rec_Wsi"]),
        "places": sample_places(),
        "dense_t": k_major(np.ascontiguousarray(a["r_dense_t"].T)),
        "wd_t": k_major(np.ascontiguousarray(a["L0_rec_Wd"].T)),
        "wl_chunks": wl,
        "picks": picks,
        "w1": k_major(np.concatenate([a["W_top1"][:USED], a["W_top1"][MAXD:]], axis=0)),
        "w2": k_major(a["W_top2"]),
    }
    nc = _bacc.Bacc("TRN2", target_bir_lowering=False, num_devices=1)
    args = []
    for name, x in arrays.items():
        arrays[name] = np.ascontiguousarray(x)
        args.append(nc.dram_tensor(name, x.shape, mybir.dt.from_np(x.dtype), kind="ExternalInput").ap())
    args.append(nc.dram_tensor("out", (1, B), mybir.dt.float32, kind="ExternalOutput").ap())
    dlrm_tower(nc, *args)
    r = _run(nc, [arrays], core_ids=[0])
    return r.results[0]["out"].reshape(B, 1)
```

```python
from contextlib import ExitStack

import numpy as np

import concourse.bass as bass
from concourse import mybir

B = 512
NF = 26
D = 64
E = 128
P = 32
MAXD, USED = 512, 384
DD = 256
H1, H2 = 512, 256
EPS = 1e-5

BT = 128
ROUNDS = B // BT
TILES = BT * NF // 128
STARTS = [0, 4, 8, 10, 14, 18, 20, 24, TILES]
GROUPS = len(STARTS) - 1
GT = 4
BANK_B = 16
BANKS = BT // BANK_B
PATTERN = 13
BLK = 6
CHUNKS = 5
ZB = BT // 4
ZK = 512 // (P + 1)
SUMS = P + 2
SQ = 8
SLOT_ROW = SQ - 1
TOPK = (USED + DD) // 128

W_LAG = 3
Z_LAG = 5
COPY_Z = Z_LAG + GROUPS
TURN_Z = COPY_Z + 1
LAYER = COPY_Z + 2, COPY_Z + 3
NORM = COPY_Z + 4
TOP1 = COPY_Z + 5, COPY_Z + 6
TOP2 = COPY_Z + 7
TOP2_OUT = COPY_Z + 8


def group_tiles(q):
    return list(range(STARTS[q], STARTS[q + 1]))


def bank_parts(m):
    mm, base = m % (BANKS // 2), PATTERN * (m // (BANKS // 2))
    parts = []
    for tt in range(BANK_B * NF * mm // 128, (BANK_B * NF * (mm + 1) - 1) // 128 + 1):
        first, last = 128 * tt // NF, (128 * tt + 127) // NF
        lo, hi = max(first, BANK_B * mm), min(last, BANK_B * mm + BANK_B - 1)
        parts.append((base + tt, tt, P * (lo - BANK_B * mm), P * (hi + 1 - BANK_B * mm), lo - first, hi + 1 - first))
    return parts


def last_bank(q):
    return max(m for m in range(BANKS) if any(p[0] in group_tiles(q) for p in bank_parts(m)))


assert all(bank_parts(m)[-1][0] in group_tiles(m) for m in range(BANKS))

VEC = {}
for _name, _n in (("gs", 1), ("gd", 1), ("bd", 1), ("gl", USED // 128), ("bl", USED // 128), ("b1", H1 // 128),
                  ("b2", H2 // 128), ("w3", H2 // 128), ("g_i", CHUNKS), ("g_j", CHUNKS), ("b_i", CHUNKS),
                  ("b_j", CHUNKS)):
    VEC[_name] = (sum(n for _, n in VEC.values()), _n)
NVEC = sum(n for _, n in VEC.values())


def dlrm_tower(nc, tbl, ids, base, ident, vecs, bs_row, ws_t, wsi_rows, places, slots, dense_t, wd_t, wl_chunks, picks, w1, w2, out):
    fp32, i32 = mybir.dt.float32, mybir.dt.int32
    ALU, ACT, AX = mybir.AluOpType, mybir.ActivationFunctionType, mybir.AxisListType

    ctx = ExitStack()
    with ctx:
        def sb(name, shape, dt=fp32):
            return ctx.enter_context(nc.sbuf_tensor(name, shape, dt))

        def ps(name, shape):
            return ctx.enter_context(nc.psum_tensor(name, shape, fp32))

        def sem(name):
            return ctx.enter_context(nc.semaphore(name))

        idx = sb("idx", [128, ROUNDS * TILES], i32)
        idx_base = sb("idx_base", [128, ROUNDS * TILES], i32)
        identity = sb("identity", [128, 128])
        vec = sb("vec", [128, NVEC])
        bs_rep = sb("bs_rep", [NF, E])
        ws_raw = sb("ws_raw", [128, E])
        ws_mean = sb("ws_mean", [128, 1])
        ws_diag = sb("ws_diag", [128, 2, E])
        wsi = sb("wsi", [128, PATTERN, BLK, P])
        wsi_raw = sb("wsi_raw", [128, PATTERN, P])
        wsi_mean = sb("wsi_mean", [128, PATTERN])
        place = sb("place", [128, PATTERN, BLK])
        shift = sb("shift", [128, P])
        dense = sb("dense", [128, DD // 128, B])
        wd = sb("wd", [128, DD // 128, E])
        wl = sb("wl", [128, CHUNKS, MAXD])
        pick = sb("pick", [128, 3, CHUNKS, SUMS])
        gb = sb("gb", [128, 4, CHUNKS])
        sum_mix = sb("sum_mix", [128, CHUNKS, SUMS])
        wl_sum = sb("wl_sum", [SUMS, MAXD])
        slot = sb("slot", [SUMS, 2, 128])
        w_top1 = sb("w_top1", [128, TOPK, H1])
        w_top2 = sb("w_top2", [128, H1 // 128, H2])
        eps = sb("eps", [128, 1])

        def col(name, k=0, n=1):
            at = VEC[name][0] + k
            return vec[:, at:at + n]

        xn = sb("xn", [128, ROUNDS, E])
        x_stats = sb("x_stats", [128, ROUNDS, 6])
        x_mean_var = sb("x_mean_var", [128, ROUNDS, 2])
        x_std = sb("x_std", [128, ROUNDS])
        x_rstd = sb("x_rstd", [128, ROUNDS])
        x_t = sb("x_t", [128, B])
        emb = sb("emb", [128, TILES, D])
        emb_t = sb("emb_t", [128, 2, 2, 128])
        u_sq = sb("u_sq", [128, 2, GT, E])
        u_var = sb("u_var", [128, 2, GT])
        u_std = sb("u_std", [128, 2, GT])
        u_rstd = sb("u_rstd", [128, 2, GT])
        u_norm = sb("u_norm", [128, TILES, E])
        y = sb("y", [128, 2, BANK_B, P])
        y_sq = sb("y_sq", [128, 2, BANK_B, P])
        y_var = sb("y_var", [128, 2, BANK_B])
        y_std = sb("y_std", [128, 2, BANK_B])
        y_rstd = sb("y_rstd", [128, 2, BANK_B])
        x_sum = sb("x_sum", [128, ROUNDS])
        rows = sb("rows", [128, P + 2, BT])
        z_raw = sb("z_raw", [128, ZB, P + 1])
        z = sb("z", [128, P, P])
        z_pack = sb("z_pack", [128, CHUNKS * 128])
        z_sums = sb("z_sums", [128, SUMS])
        z_t = sb("z_t", [128, CHUNKS, BT])
        stats = sb("stats", [128, 6])
        mean_var = sb("mean_var", [128, 2])
        carrier = sb("carrier", [128, 10])
        l_std = sb("l_std", [128, 1])
        l_rstd = sb("l_rstd", [128, 1])
        l_norm = sb("l_norm", [128, USED])
        l_t = sb("l_t", [128, USED // 128, BT])
        h1 = sb("h1", [128, H1 // 128, BT])
        h2 = sb("h2", [128, H2 // 128, B])
        y_out = sb("y_out", [1, B])

        ps_u = [ps(f"ps_u{i}", [128, GT, E]) for i in range(2)]
        ps_y = [ps(f"ps_y{i}", [128, BANK_B, P]) for i in range(2)]
        ps_z = ps("ps_z", [128, 3, 512])
        ps_p = ps("ps_p", [128, 512])

        ids_in, base_in, ident_in, vec_in, bs_in = (sem(n) for n in ("ids_in", "base_in", "ident_in", "vec_in", "bs_in"))
        ws_in, wsi_in, dense_in, wd_in = (sem(n) for n in ("ws_in", "wsi_in", "dense_in", "wd_in"))
        wl_in, pick_in, w1_in, w2_in = (sem(n) for n in ("wl_in", "pick_in", "w1_in", "w2_in"))
        slot_in, placed_mm = sem("slot_in"), sem("placed_mm")
        gb_ready, mix_step, sum_mm, wl_sum_ready, wl_scaled = (
            sem(n) for n in ("gb_ready", "mix_step", "sum_mm", "wl_sum_ready", "wl_scaled"))
        idx_ready = sem("idx_ready")
        gathered = [sem(f"gathered{q}") for q in range(GROUPS)]
        filled = sem("filled")
        ws_step, wsi_step = sem("ws_step"), sem("wsi_step")
        shift_mm, shift_ready, sx_mm, sx_ready = (sem(n) for n in ("shift_mm", "shift_ready", "sx_mm", "sx_ready"))
        x_mm, x_stat, x_aggr, x_root, x_inv, x_norm, x_tr, x_ready = (
            sem(n) for n in ("x_mm", "x_stat", "x_aggr", "x_root", "x_inv", "x_norm", "x_tr", "x_ready"))
        emb_turned, emb_copied = sem("emb_turned"), sem("emb_copied")
        u_mm, u_squared, u_root, u_inv, u_scaled = (
            sem(n) for n in ("u_mm", "u_squared", "u_root", "u_inv", "u_scaled"))
        y_mm, y_shifted, y_squared, y_summed, y_root, y_inv, y_scaled = (
            sem(n) for n in ("y_mm", "y_shifted", "y_squared", "y_summed", "y_root", "y_inv", "y_scaled"))
        x_placed, z_mm, z_copied, sx_copied, z_ready, z_squared, z_packed = (
            sem(n) for n in ("x_placed", "z_mm", "z_copied", "sx_copied", "z_ready", "z_squared", "z_packed"))
        z_turned, zt_copied, l_mm, l_stat, l_aggr, l_root, l_inv, l_scaled, l_turned, lt_ready = (
            sem(n) for n in ("z_turned", "zt_copied", "l_mm", "l_stat", "l_aggr", "l_root", "l_inv", "l_scaled",
                             "l_turned", "lt_ready"))
        late_h1_mm, late_h1_ready, late_h2_mm, late_h2_ready = (
            sem(n) for n in ("late_h1_mm", "late_h1_ready", "late_h2_mm", "late_h2_ready"))
        h1_mm, h1_ready, h2_mm, h2_ready, out_mm, out_copied, stored = (
            sem(n) for n in ("h1_mm", "h1_ready", "h2_mm", "h2_ready", "out_mm", "out_copied", "stored"))

        def live(t):
            return not isinstance(t[0], int) or 0 <= t[0] + t[1] < ROUNDS

        def count(per_round, t, n):
            return t[0] * per_round + (t[1] * per_round + n)

        def past(per_round, t, n):
            return count(per_round, t, n + 1)

        def wait(eng, s, n):
            if not isinstance(n, int) or n > 0:
                eng.wait_ge(s, n)

        def in_rounds(t):
            return live((t[0], 0))

        def after(t, q, s):
            return isinstance(t[0], int) and (t[0], q) == (ROUNDS - 1 + s // GROUPS, s % GROUPS)

        def due(t, q, s):
            r = (t[0], t[1] - s // GROUPS)
            return r if q == s % GROUPS and live(r) else None

        def first(t):
            return isinstance(t[0], int) and t[0] == 0

        def second(t):
            return isinstance(t[0], int) and t[0] == 1

        def at(t, q, lag):
            return (t[0], t[1] + (q - lag) // GROUPS), (q - lag) % GROUPS

        def z_cols(bb):
            at = (P + 1) * (bb % ZK)
            return bb // ZK, slice(at, at + P + 1)

        def run(eng, step):
            for r in range(2):
                for q in range(GROUPS):
                    step((r, 0), q)
            with eng.Fori(2, ROUNDS) as t:
                for q in range(GROUPS):
                    step((t, 0), q)
            for r in range(ROUNDS, ROUNDS + 2):
                for q in range(GROUPS):
                    step((r, 0), q)

        LATE = (ROUNDS - 2, ROUNDS - 1)
        LAYER_K, DENSE_K = tuple(range(USED // 128)), tuple(range(USED // 128, TOPK))

        def late_bank(c):
            return ps_u[c][:, 0, :] if c < 2 else ps_y[c - 2][:, 0:BT // P, :].rearrange("p a b -> p (a b)")

        block = ctx.enter_context(nc.Block())

        @block.sync
        def _(sp):
            sp.dma_start(idx[:, :], ids).then_inc(ids_in, 16)
            sp.dma_start(idx_base[:, :], base).then_inc(base_in, 16)
            sp.dma_start(ws_raw[:, :], ws_t).then_inc(ws_in, 16)
            sp.dma_start(wsi_raw[:, :, :], wsi_rows).then_inc(wsi_in, 16)
            sp.dma_start(place[:, :, :], places).then_inc(wsi_in, 16)
            sp.dma_start(identity[:, :], ident).then_inc(ident_in, 16)
            sp.dma_start(wd[:, :, :], wd_t).then_inc(wd_in, 16)
            sp.dma_start(dense[:, :, :], dense_t).then_inc(dense_in, 16)
            sp.dma_start(vec[:, :], vecs).then_inc(vec_in, 16)
            sp.dma_start(bs_rep[:, :], bs_row).then_inc(bs_in, 16)
            sp.wait_ge(gathered[0], 16 * len(group_tiles(0)))
            sp.dma_start(pick[:, :, :, :], picks).then_inc(pick_in, 16)
            sp.dma_start(slot[:, :, :], slots).then_inc(slot_in, 16)
            sp.wait_ge(gathered[2], 16 * len(group_tiles(2)))
            sp.dma_start(wl[:, :, :], wl_chunks).then_inc(wl_in, 16)
            sp.wait_ge(gathered[4], 16 * len(group_tiles(4)))
            sp.dma_start(w_top1[:, :, :], w1).then_inc(w1_in, 16)
            sp.wait_ge(gathered[6], 16 * len(group_tiles(6)))
            sp.dma_start(w_top2[:, :, :], w2).then_inc(w2_in, 16)
            sp.wait_ge(out_copied, 2)
            sp.dma_start(out, y_out[:, :]).then_inc(stored, 16)
            sp.wait_ge(stored, 16)

        @block.gpsimd
        def _(pool):
            pool.wait_ge(idx_ready, 1)
            for t in range(ROUNDS):
                for q in range(GROUPS):
                    wait(pool, emb_turned, GROUPS * (t - 1) + q + 1)
                    for k in group_tiles(q):
                        g = TILES * t + k
                        pool.indirect_dma_start(
                            emb[:, k, :], None, tbl, bass.IndirectOffsetOnAxis(ap=idx[:, g:g + 1], axis=0),
                        ).then_inc(gathered[q], 16)

        @block.tensor
        def _(pe):
            def project_dense(rounds):
                pe.wait_ge(dense_in, 16)
                pe.wait_ge(wd_in, 16)
                for r in rounds:
                    for k in range(DD // 128):
                        mm = nc.tensor.matmul(ps_p[:, E * r:E * (r + 1)], dense[:, k, BT * r:BT * (r + 1)], wd[:, k, :],
                                              start=(k == 0), stop=(k == DD // 128 - 1))
                if rounds[-1] == ROUNDS - 1:
                    mm.then_inc(x_mm, 1)

            def turn_dense():
                pe.wait_ge(x_norm, 1)
                for r in range(ROUNDS):
                    mm = nc.tensor.transpose(ps_p[:, BT * r:BT * (r + 1)], xn[:, r, :], identity[:, :])
                mm.then_inc(x_tr, 1)

            def bias_row():
                pe.wait_ge(bs_in, 16)
                pe.wait_ge(wsi_step, 3)
                nc.tensor.matmul(ps_z[:, 0, 0:P], bs_rep[:, :], wsi[0:NF, 0, 0, :], start=True, stop=True).then_inc(shift_mm, 1)

            def sum_dense():
                pe.wait_ge(x_ready, 1)
                pe.wait_ge(filled, 4)
                for r in range(ROUNDS):
                    mm = nc.tensor.matmul(ps_p[:, r:r + 1], x_t[:, BT * r:BT * (r + 1)], rows[:, 0, 0:1],
                                          start=True, stop=True)
                mm.then_inc(sx_mm, 1)

            def weights_of_sums(chunks):
                if chunks[0] == 0:
                    pe.wait_ge(sx_ready, 1)
                    pe.wait_ge(wl_in, 16)
                    pe.wait_ge(mix_step, 3 * CHUNKS)
                for c in chunks:
                    nc.tensor.matmul(ps_p[0:SUMS, :], sum_mix[:, c, :], wl[:, c, :], start=(c == 0),
                                     stop=(c == CHUNKS - 1)).then_inc(sum_mm, 1)

            def place_sums(c):
                pe.wait_ge(wl_sum_ready, 1)
                pe.wait_ge(slot_in, 16)
                if c == CHUNKS - 1:
                    pe.wait_ge(wl_scaled, CHUNKS - 1)
                nc.tensor.matmul(ps_p[:, :], slot[:, c - (CHUNKS - 2), :], wl_sum[:, :], start=True,
                                 stop=True).then_inc(placed_mm, 1)

            def turn_gathers(t, q):
                pe.wait_ge(gathered[q], count(16 * len(group_tiles(q)), t, 16 * len(group_tiles(q))))
                wait(pe, u_scaled, count(GROUPS, t, q - 1))
                for i, k in enumerate(group_tiles(q)[::2]):
                    mm = nc.tensor.transpose(ps_u[q % 2][:, i, :],
                                             emb[:, k:k + 2, :].rearrange("p k d -> p (k d)"), identity[:, :])
                mm.then_inc(emb_turned, 1)

            def project(t, q):
                pe.wait_ge(emb_copied, count(GROUPS, t, q + 1))
                for i in range(len(group_tiles(q)) // 2):
                    mm = nc.tensor.matmul(ps_u[q % 2][:, 2 * i:2 * i + 2, :], emb_t[:, q % 2, i, :], ws_diag[:, :, :],
                                          start=True, stop=True)
                mm.then_inc(u_mm, 1)

            def mix_features(t, m):
                pe.wait_ge(u_scaled, count(GROUPS, t, m + 1))
                wait(pe, y_shifted, count(BANKS, t, m - 1))
                parts = bank_parts(m)
                flat = ps_y[m % 2][:, :, :].rearrange("p b r -> p (b r)")
                for n, (tile, tt, lo, hi, b0, b1) in enumerate(parts):
                    mm = nc.tensor.matmul(flat[:, lo:hi], u_norm[:, tile, :], wsi[:, tt, b0:b1, :],
                                          start=(n == 0), stop=(n == len(parts) - 1), skip_group_check=True)
                mm.then_inc(y_mm, 1)

            def pairs(t, m):
                pe.wait_ge(y_scaled, count(BANKS, t, m + 1))
                if m == 0:
                    pe.wait_ge(x_placed, count(1, t, 1))
                    wait(pe, z_copied, count(1, t, 0))
                for b in range(BANK_B * m, BANK_B * (m + 1)):
                    quarter, bb = b // 32, b % 32
                    bank, cols = z_cols(bb)
                    mm = nc.tensor.matmul(ps_z[32 * quarter:32 * quarter + 32, bank, cols], rows[:, 2:P + 2, b],
                                          rows[:, 0:P + 1, b], start=True, stop=True)
                mm.then_inc(z_mm, 1)

            def turn_pairs(t, chunks):
                if chunks[0] == 0:
                    if in_rounds(t):
                        wait(pe, h2_ready, count(1, t, 0))
                    else:
                        pe.wait_ge(lt_ready, LATE[1])
                    pe.wait_ge(z_packed, past(1, t, 1))
                else:
                    pe.wait_ge(zt_copied, count(2, t, 1))
                for i, c in enumerate(chunks):
                    mm = nc.tensor.transpose(ps_p[:, BT * i:BT * (i + 1)], z_pack[:, 128 * c:128 * (c + 1)], identity[:, :])
                mm.then_inc(z_turned, 1)

            def interaction_layer(t, chunks):
                if chunks[0] == 0:
                    pe.wait_ge(zt_copied, count(2, t, 2))
                    pe.wait_ge(wl_scaled, CHUNKS)
                for c in chunks:
                    mm = nc.tensor.matmul(ps_p[:, :], z_t[:, c, :], wl[:, c, :], start=(c == 0), stop=(c == CHUNKS - 1))
                if chunks[-1] == CHUNKS - 1:
                    mm.then_inc(l_mm, 1)

            def turn_layer(t):
                pe.wait_ge(l_scaled, count(1, t, 1))
                for c in range(USED // 128):
                    mm = nc.tensor.transpose(ps_p[:, BT * c:BT * (c + 1)], l_norm[:, 128 * c:128 * (c + 1)], identity[:, :])
                mm.then_inc(l_turned, 1)

            def top1(t, chunks):
                if chunks[0] == 0:
                    pe.wait_ge(w1_in, 16)
                    pe.wait_ge(lt_ready, count(1, t, 1))
                for c in chunks:
                    for k in range(TOPK):
                        kd = k - USED // 128
                        mm = nc.tensor.matmul(ps_p[:, BT * c:BT * (c + 1)], w_top1[:, k, 128 * c:128 * (c + 1)],
                                              l_t[:, k, :] if kd < 0 else dense[:, kd, bass.ds((t[0] + t[1]) * BT, BT)],
                                              start=(k == 0), stop=(k == TOPK - 1))
                mm.then_inc(h1_mm, 1)

            def top2(t):
                pe.wait_ge(w2_in, 16)
                pe.wait_ge(h1_ready, count(1, t, 1))
                for c in range(H2 // 128):
                    for k in range(H1 // 128):
                        mm = nc.tensor.matmul(ps_p[:, BT * c:BT * (c + 1)], w_top2[:, k, 128 * c:128 * (c + 1)],
                                              h1[:, k, :], start=(k == 0), stop=(k == H1 // 128 - 1))
                mm.then_inc(h2_mm, 1)

            def late_top1(late, ks, chunks=range(H1 // 128)):
                r = LATE[late]
                if ks[0] == DENSE_K[0]:
                    pe.wait_ge(u_scaled, GROUPS * ROUNDS)
                    if chunks[-1] >= 2:
                        pe.wait_ge(y_shifted, BANKS * ROUNDS)
                    wait(pe, late_h1_ready, 4 * late)
                if ks[-1] == LAYER_K[-1]:
                    pe.wait_ge(lt_ready, r + 1)
                for c in chunks:
                    for k in ks:
                        kd = k - USED // 128
                        mm = nc.tensor.matmul(late_bank(c), w_top1[:, k, 128 * c:128 * (c + 1)],
                                              l_t[:, k, :] if kd < 0 else dense[:, kd, BT * r:BT * (r + 1)],
                                              start=(k == DENSE_K[0]), stop=(k == LAYER_K[-1]))
                    if ks[-1] == LAYER_K[-1]:
                        mm.then_inc(late_h1_mm, 1)

            def late_top2(late, ks=range(H1 // 128)):
                if ks[0] == 0:
                    if late == 0:
                        pe.wait_ge(z_copied, ROUNDS)
                    else:
                        pe.wait_ge(late_h2_ready, 1)
                for k in ks:
                    pe.wait_ge(late_h1_ready, H1 // 128 * late + k + 1)
                    for c in range(H2 // 128):
                        mm = nc.tensor.matmul(ps_z[:, c, 0:BT], w_top2[:, k, 128 * c:128 * (c + 1)], h1[:, k, :],
                                              start=(k == 0), stop=(k == H1 // 128 - 1))
                if ks[-1] == H1 // 128 - 1:
                    mm.then_inc(late_h2_mm, 1)

            def output(b0, b1):
                for k in range(H2 // 128):
                    mm = nc.tensor.matmul(ps_z[0:1, 2, b0:b1], col("w3", k), h2[:, k, b0:b1],
                                          start=(k == 0), stop=(k == H2 // 128 - 1))
                mm.then_inc(out_mm, 1)

            def early_top3():
                pe.wait_ge(h2_ready, LATE[0])
                pe.wait_ge(late_h2_ready, 1)
                output(0, BT * LATE[1])

            def top3():
                pe.wait_ge(late_h2_ready, 2)
                pe.wait_ge(out_copied, 1)
                output(BT * LATE[1], B)

            def step(t, q):
                if (r := at(t, q, 1)) and live(r[0]):
                    project(*r)
                if r := due(t, q, LAYER[1]):
                    interaction_layer(r, (3,))
                if (r := at(t, q, W_LAG)) and live(r[0]):
                    mix_features(*r)
                if after(t, q, TURN_Z):
                    late_top2(0, (0, 1))
                if r := due(t, q, TURN_Z):
                    turn_pairs(r, (0, 1, 2, 3))
                if r := due(t, q, LAYER[0]):
                    interaction_layer(r, (0, 1))
                if r := due(t, q, LAYER[1]):
                    interaction_layer(r, (4,))
                if live(t):
                    turn_gathers(t, q)
                if after(t, q, COPY_Z - 3):
                    late_top1(0, LAYER_K, (0,))
                if after(t, q, COPY_Z - 2):
                    late_top1(0, LAYER_K, (1,))
                if (r := at(t, q, Z_LAG)) and live(r[0]):
                    pairs(*r)
                if after(t, q, COPY_Z - 4):
                    late_top1(0, DENSE_K, (0, 1))
                if after(t, q, COPY_Z - 1):
                    late_top1(0, DENSE_K + LAYER_K, (2, 3))
                if after(t, q, TURN_Z):
                    late_top2(0, (2, 3))
                if after(t, q, NORM):
                    late_top1(1, DENSE_K)
                if r := due(t, q, TURN_Z):
                    turn_pairs(r, (4,))
                if r := due(t, q, LAYER[0]):
                    interaction_layer(r, (2,))
                if r := due(t, q, NORM):
                    turn_layer(r)
                if after(t, q, NORM):
                    early_top3()
                if in_rounds(t):
                    if r := due(t, q, TOP1[0]):
                        top1(r, (0, 1))
                    if r := due(t, q, TOP1[1]):
                        top1(r, (2, 3))
                    if r := due(t, q, TOP2):
                        top2(r)
                if first(t):
                    if q == 0:
                        project_dense((2, 3))
                        bias_row()
                    if q == 1:
                        turn_dense()
                    if q == 2:
                        sum_dense()
                    if q == 4:
                        weights_of_sums((0, 1))
                    if q == 5:
                        weights_of_sums((2, 3))
                    if q == 6:
                        weights_of_sums((4,))
                    if q == 7:
                        place_sums(3)
                if second(t) and q == 1:
                    place_sums(4)

            pe.wait_ge(ident_in, 16)
            pe.wait_ge(ws_step, 3)
            project_dense((0, 1))
            run(pe, step)
            pe.wait_ge(vec_in, 16)
            late_top1(1, LAYER_K)
            late_top2(1)
            top3()

        @block.scalar
        def _(act):
            act.wait_ge(filled, 1)
            nc.scalar.activation(l_std[:, :], eps[:, :], ACT.Sqrt)

            def root_dense():
                act.wait_ge(x_aggr, ROUNDS)
                nc.scalar.activation(x_std[:, :], x_mean_var[:, :, 1], ACT.Sqrt, bias=eps[:, :]).then_inc(x_root, 1)

            def scale_dense():
                act.wait_ge(vec_in, 16)
                act.wait_ge(x_tr, 1)
                nc.scalar.activation(x_t[:, :], ps_p[:, :], ACT.Identity, bias=col("bd"), scale=col("gd")).then_inc(x_ready, 1)

            def copy_bias_row():
                act.wait_ge(shift_mm, 1)
                nc.scalar.copy(shift[:, :], ps_z[:, 0, 0:P]).then_inc(shift_ready, 1)

            def copy_dense_sums():
                act.wait_ge(sx_mm, 1)
                nc.scalar.copy(x_sum[:, :], ps_p[:, 0:ROUNDS]).then_inc(sx_ready, 1)

            def copy_weights_of_sums():
                act.wait_ge(sum_mm, CHUNKS)
                nc.scalar.copy(wl_sum[:, :], ps_p[0:SUMS, :]).then_inc(wl_sum_ready, 1)

            def copy_gathers(t, q):
                n = len(group_tiles(q)) // 2
                act.wait_ge(emb_turned, count(GROUPS, t, q + 1))
                wait(act, u_mm, count(GROUPS, t, q - 1))
                nc.scalar.copy(emb_t[:, q % 2, 0:n, :], ps_u[q % 2][:, 0:n, :]).then_inc(emb_copied, 1)

            def square_u(t, q):
                n = len(group_tiles(q))
                act.wait_ge(u_mm, count(GROUPS, t, q + 1))
                for k in range(n):
                    a = nc.scalar.activation(u_sq[:, q % 2, k, :], ps_u[q % 2][:, k, :], ACT.Square,
                                             accum_out=u_var[:, q % 2, k:k + 1])
                a.then_inc(u_squared, 1)

            def root_u(t, q):
                n = len(group_tiles(q))
                act.wait_ge(u_squared, count(GROUPS, t, q + 1))
                wait(act, u_inv, count(GROUPS, t, q - 1))
                nc.scalar.activation(u_std[:, q % 2, 0:n], u_var[:, q % 2, 0:n], ACT.Sqrt, bias=eps[:, :],
                                     scale=1.0 / E).then_inc(u_root, 1)

            def square_y(t, m):
                act.wait_ge(y_shifted, count(BANKS, t, m + 1))
                wait(act, y_summed, count(BANKS, t, m - 1))
                nc.scalar.activation(y_sq[:, m % 2, :, :], y[:, m % 2, :, :], ACT.Square).then_inc(y_squared, 1)

            def root_y(t, m):
                act.wait_ge(y_summed, count(BANKS, t, m + 1))
                wait(act, y_inv, count(BANKS, t, m - 1))
                nc.scalar.activation(y_std[:, m % 2, :], y_var[:, m % 2, :], ACT.Sqrt, bias=eps[:, :],
                                     scale=1.0 / P).then_inc(y_root, 1)

            def place_x(t):
                wait(act, z_mm, past(BANKS, t, 0))
                nc.scalar.copy(rows[:, 1, :], x_t[:, bass.ds((t[0] + t[1]) * BT, BT)]).then_inc(x_placed, 1)

            def copy_z(t):
                act.wait_ge(z_mm, past(BANKS, t, BANKS))
                wait(act, z_ready, past(1, t, 0))
                for first in range(0, ZB, ZK):
                    n = min(ZK, ZB - first)
                    a = nc.scalar.copy(z_raw[:, first:first + n, :], ps_z[:, first // ZK, 0:n * (P + 1)].rearrange(
                        "p (b j) -> p b j", b=n))
                a.then_inc(z_copied, 1)
                wait(act, z_packed, past(1, t, 0))
                nc.scalar.copy(z_sums[:, P:P + 1], x_sum[:, bass.ds(t[0] + t[1], 1)]).then_inc(sx_copied, 1)

            def copy_pairs(t, n):
                act.wait_ge(z_turned, past(2, t, n + 1))
                wait(act, l_mm, past(1, t, 0))
                if n == 0:
                    nc.scalar.copy(z_t[:, 0:4, :], ps_p[:, :].rearrange("p (k b) -> p k b", k=4)).then_inc(zt_copied, 1)
                else:
                    nc.scalar.copy(z_t[:, 4, :], ps_p[:, 0:BT]).then_inc(zt_copied, 1)

            def root_l(t):
                act.wait_ge(l_aggr, count(1, t, 1))
                nc.scalar.activation(l_std[:, :], mean_var[:, 1:2], ACT.Sqrt, bias=eps[:, :]).then_inc(l_root, 1)

            def scale_l(t):
                act.wait_ge(l_turned, count(1, t, 1))
                if not isinstance(t[0], int) or t[0] + t[1] < LATE[1]:
                    wait(act, h1_mm, past(2, t, 0))
                else:
                    act.wait_ge(late_h1_mm, H1 // 128)
                for c in range(USED // 128):
                    a = nc.scalar.activation(l_t[:, c, :], ps_p[:, BT * c:BT * (c + 1)], ACT.Identity, bias=col("bl", c),
                                             scale=col("gl", c))
                a.then_inc(lt_ready, 1)

            def relu1(t):
                act.wait_ge(h1_mm, past(2, t, 2))
                wait(act, h2_mm, past(1, t, 0))
                for c in range(H1 // 128):
                    a = nc.scalar.activation(h1[:, c, :], ps_p[:, BT * c:BT * (c + 1)], ACT.Relu, bias=col("b1", c))
                a.then_inc(h1_ready, 1)

            def relu2(t):
                act.wait_ge(h2_mm, past(1, t, 1))
                for c in range(H2 // 128):
                    a = nc.scalar.activation(h2[:, c, bass.ds((t[0] + t[1]) * BT, BT)], ps_p[:, BT * c:BT * (c + 1)],
                                             ACT.Relu, bias=col("b2", c))
                a.then_inc(h2_ready, 1)

            def relu1_late(late, chunks=range(H1 // 128)):
                if late == 0:
                    act.wait_ge(h2_mm, 1 + LATE[0])
                else:
                    act.wait_ge(late_h2_mm, 1)
                for c in chunks:
                    act.wait_ge(late_h1_mm, H1 // 128 * late + c + 1)
                    nc.scalar.activation(h1[:, c, :], late_bank(c), ACT.Relu, bias=col("b1", c)).then_inc(late_h1_ready, 1)

            def relu2_late(late):
                r = LATE[late]
                act.wait_ge(late_h2_mm, late + 1)
                for c in range(H2 // 128):
                    a = nc.scalar.activation(h2[:, c, BT * r:BT * (r + 1)], ps_z[:, c, 0:BT], ACT.Relu, bias=col("b2", c))
                a.then_inc(late_h2_ready, 1)

            def step(t, q):
                if r := due(t, q, COPY_Z):
                    copy_z(r)
                if r := due(t, q, LAYER[0]):
                    copy_pairs(r, 1)
                if live(t) and q == Z_LAG:
                    place_x(t)
                if in_rounds(t) and (r := due(t, q, TOP2)):
                    relu1(r)
                if (r := at(t, q, 1)) and live(r[0]):
                    square_u(*r)
                    root_u(*r)
                if r := due(t, q, TURN_Z):
                    copy_pairs(r, 0)
                if live(t):
                    copy_gathers(t, q)
                if (r := at(t, q, W_LAG + 1)) and live(r[0]):
                    root_y(*r)
                if r := due(t, q, LAYER[1]):
                    root_l(r)
                if in_rounds(t) and (r := due(t, q, TOP2_OUT)):
                    relu2(r)
                if (r := at(t, q, W_LAG)) and live(r[0]):
                    square_y(*r)
                if r := due(t, q, NORM):
                    scale_l(r)
                if after(t, q, COPY_Z - 1):
                    relu1_late(0, (0, 1))
                if after(t, q, COPY_Z):
                    relu1_late(0, (2, 3))
                if after(t, q, LAYER[0]):
                    relu2_late(0)
                if first(t):
                    if q == 0:
                        root_dense()
                        copy_bias_row()
                    if q == 1:
                        scale_dense()
                    if q == 2:
                        copy_dense_sums()
                    if q == 6:
                        copy_weights_of_sums()

            run(act, step)
            relu1_late(1)
            act.wait_ge(out_mm, 1)
            nc.scalar.copy(y_out[:, 0:BT * LATE[1]], ps_z[0:1, 2, 0:BT * LATE[1]]).then_inc(out_copied, 1)
            relu2_late(1)
            act.wait_ge(out_mm, 2)
            nc.scalar.copy(y_out[:, BT * LATE[1]:], ps_z[0:1, 2, BT * LATE[1]:]).then_inc(out_copied, 1)

        @block.vector
        def _(dve):
            nc.vector.memset(eps[:, :], EPS).then_inc(filled, 1)
            nc.vector.memset(ws_diag[:, :, :], 0.0).then_inc(filled, 1)
            nc.vector.memset(rows[:, 0, :], 1.0).then_inc(filled, 1)
            nc.vector.memset(z_sums[:, P + 1:], 1.0).then_inc(filled, 1)
            for n, s in enumerate((y_mm, z_mm, z_ready, z_packed, z_turned, l_mm, h1_mm, h2_mm)):
                nc.vector.memset(carrier[:, 1 + n:2 + n], 0.0).then_inc(s, 1)
            dve.wait_ge(ids_in, 16)
            dve.wait_ge(base_in, 16)
            nc.vector.tensor_tensor(idx[:, :], idx[:, :], idx_base[:, :], ALU.add).then_inc(idx_ready, 1)
            dve.wait_ge(ws_in, 16)
            nc.vector.tensor_reduce(ws_mean[:, :], ws_raw[:, :], AX.X, ALU.add).then_inc(ws_step, 1)
            dve.wait_ge(ws_step, 1)
            nc.vector.tensor_scalar(ws_mean[:, :], ws_mean[:, :], 1.0 / E, None, ALU.mult).then_inc(ws_step, 1)
            dve.wait_ge(ws_step, 2)
            dve.wait_ge(filled, 2)
            for half in range(2):
                rows_of = slice(D * half, D * (half + 1))
                c = nc.vector.tensor_scalar(ws_diag[rows_of, half, :], ws_raw[rows_of, :], ws_mean[rows_of, :], None,
                                            ALU.subtract)
            c.then_inc(ws_step, 1)

            def place_wsi():
                dve.wait_ge(wsi_in, 32)
                nc.vector.tensor_reduce(wsi_mean[:, :], wsi_raw[:, :, :], AX.X, ALU.add).then_inc(wsi_step, 1)
                dve.wait_ge(wsi_step, 1)
                nc.vector.scalar_tensor_tensor(wsi_raw[:, :, :], wsi_mean[:, :].unsqueeze(2).broadcast_to([128, PATTERN, P]),
                                               -1.0 / P, wsi_raw[:, :, :], ALU.mult, ALU.add).then_inc(wsi_step, 1)
                dve.wait_ge(wsi_step, 2)
                for b in range(BLK):
                    a = nc.vector.tensor_tensor(wsi[:, :, b, :], wsi_raw[:, :, :],
                                                place[:, :, b:b + 1].broadcast_to([128, PATTERN, P]), ALU.mult)
                a.then_inc(wsi_step, 1)

            def norm_dense():
                dve.wait_ge(x_mm, 1)
                for r in range(ROUNDS):
                    nc.vector.bn_stats(x_stats[:, r, :], ps_p[:, E * r:E * (r + 1)]).then_inc(x_stat, 1)
                for r in range(ROUNDS):
                    dve.wait_ge(x_stat, r + 1)
                    nc.vector.bn_aggr(x_mean_var[:, r, :], x_stats[:, r, :]).then_inc(x_aggr, 1)

            def scale_dense():
                dve.wait_ge(x_root, 1)
                nc.vector.reciprocal(x_rstd[:, :], x_std[:, :]).then_inc(x_inv, 1)
                dve.wait_ge(x_inv, 1)
                for r in range(ROUNDS):
                    a = nc.vector.tensor_scalar(xn[:, r, :], ps_p[:, E * r:E * (r + 1)], x_mean_var[:, r, 0:1],
                                                x_rstd[:, r:r + 1], ALU.subtract, ALU.mult)
                a.then_inc(x_norm, 1)

            def mix_gsi_bsi():
                dve.wait_ge(vec_in, 16)
                dve.wait_ge(pick_in, 16)
                for n, (a, b) in enumerate((("g_i", "b_j"), ("g_j", "b_i"), ("b_i", "b_j"), ("g_i", "g_j"))):
                    nc.vector.scalar_tensor_tensor(gb[:, n, :], col(a, 0, CHUNKS), float(E) if n == 2 else 1.0,
                                                   col(b, 0, CHUNKS), ALU.mult, ALU.mult).then_inc(gb_ready, 1)
                dve.wait_ge(gb_ready, 4)
                for c in range(CHUNKS):
                    nc.vector.tensor_scalar(sum_mix[:, c, :], pick[:, 0, c, :], gb[:, 0, c:c + 1], None,
                                            ALU.mult).then_inc(mix_step, 1)
                for n in (1, 2):
                    dve.wait_ge(mix_step, n * CHUNKS)
                    for c in range(CHUNKS):
                        nc.vector.scalar_tensor_tensor(sum_mix[:, c, :], pick[:, n, c, :], gb[:, n, c:c + 1],
                                                       sum_mix[:, c, :], ALU.mult, ALU.add).then_inc(mix_step, 1)

            def scale_wl(chunks):
                for c in chunks:
                    dve.wait_ge(sum_mm, c + 1)
                    nc.vector.tensor_scalar(wl[:, c, :], wl[:, c, :], gb[:, 3, c:c + 1], None, ALU.mult).then_inc(wl_scaled, 1)

            def scale_wl_beside_sums(c):
                dve.wait_ge(sum_mm, c + 1)
                dve.wait_ge(placed_mm, c - (CHUNKS - 2) + 1)
                nc.vector.scalar_tensor_tensor(wl[:, c, :], wl[:, c, :], gb[:, 3, c:c + 1], ps_p[:, :], ALU.mult,
                                               ALU.add).then_inc(wl_scaled, 1)

            def invert_u(t, q):
                n = len(group_tiles(q))
                dve.wait_ge(u_root, count(GROUPS, t, q + 1))
                nc.vector.reciprocal(u_rstd[:, q % 2, 0:n], u_std[:, q % 2, 0:n]).then_inc(u_inv, 1)

            def scale_u(t, q):
                n, k = len(group_tiles(q)), STARTS[q]
                dve.wait_ge(u_inv, count(GROUPS, t, q + 1))
                wait(dve, y_mm, past(BANKS, t, last_bank(q) + 1 - BANKS))
                nc.vector.tensor_tensor(u_norm[:, k:k + n, :], ps_u[q % 2][:, 0:n, :],
                                        u_rstd[:, q % 2, 0:n].unsqueeze(2).broadcast_to([128, n, E]), ALU.mult).then_inc(u_scaled, 1)

            def shift_y(t, m):
                dve.wait_ge(y_mm, past(BANKS, t, m + 1))
                wait(dve, y_scaled, count(BANKS, t, m - 1))
                nc.vector.scalar_tensor_tensor(y[:, m % 2, :, :], ps_y[m % 2][:, :, :], col("gs"),
                                               shift[:, :].unsqueeze(1).broadcast_to([128, BANK_B, P]),
                                               ALU.mult, ALU.add).then_inc(y_shifted, 1)

            def sum_y(t, m):
                dve.wait_ge(y_squared, count(BANKS, t, m + 1))
                wait(dve, y_root, count(BANKS, t, m - 1))
                nc.vector.tensor_reduce(y_var[:, m % 2, :], y_sq[:, m % 2, :, :], AX.X, ALU.add).then_inc(y_summed, 1)

            def invert_y(t, m):
                dve.wait_ge(y_root, count(BANKS, t, m + 1))
                nc.vector.reciprocal(y_rstd[:, m % 2, :], y_std[:, m % 2, :]).then_inc(y_inv, 1)

            def scale_y(t, m):
                b0 = BANK_B * m
                dve.wait_ge(y_inv, count(BANKS, t, m + 1))
                wait(dve, z_mm, past(BANKS, t, m + 1 - BANKS))
                nc.vector.tensor_tensor(rows[:, 2:P + 2, b0:b0 + BANK_B].rearrange("e r b -> e b r"),
                                        y[:, m % 2, :, :], y_rstd[:, m % 2, :].unsqueeze(2).broadcast_to([128, BANK_B, P]),
                                        ALU.mult).then_inc(y_scaled, 1)

            def turn_z(t):
                dve.wait_ge(z_copied, count(1, t, 1))
                wait(dve, z_packed, past(1, t, 0))
                nc.vector.transpose(z[:, :, :], z_raw[:, :, 1:P + 1].rearrange("p b j -> p j b"))
                nc.vector.transpose(z_sums[:, 0:P], z_raw[:, :, 0]).then_inc(z_ready, 1)
                wait(dve, z_turned, past(2, t, 0))
                dve.wait_ge(z_ready, past(1, t, 1))

                def squares(first, step, n):
                    s = z[:, :, :]
                    return bass.AP(s.tensor, s.offset + first, [list(s.ap[0]), [step, n], [P, 8], [1, 8]])

                def packed(c, n):
                    return z_pack[:, 128 * c:128 * (c + n)].rearrange("b (s j i) -> b s j i", j=8, i=8)

                nc.vector.tensor_copy(z_pack[:, 0:256].rearrange("b (j i) -> b j i", j=16), z[:, 0:16, 16:32])
                nc.vector.tensor_copy(packed(2, 1), squares(8, 16 * P + 16, 2))
                nc.vector.tensor_copy(packed(3, 2), squares(0, 8 * P + 8, 4)).then_inc(z_squared, 1)
                dve.wait_ge(sx_copied, count(1, t, 1))
                dve.wait_ge(z_squared, count(1, t, 1))
                diagonal = z_pack[:, 128 * (CHUNKS - 2):].rearrange("b (s j i) -> b s j i", j=SQ, i=SQ)
                nc.vector.tensor_copy(diagonal[:, :, SQ - 1, 0:SLOT_ROW],
                                      z_sums[:, 0:4 * SLOT_ROW].rearrange("b (s i) -> b s i", s=4))
                nc.vector.tensor_copy(diagonal[:, 0, SQ - 2, 0:SUMS - 4 * SLOT_ROW],
                                      z_sums[:, 4 * SLOT_ROW:]).then_inc(z_packed, 1)

            def stats_l(t):
                dve.wait_ge(l_mm, past(1, t, 1))
                nc.vector.bn_stats(stats[:, :], ps_p[:, :]).then_inc(l_stat, 1)
                dve.wait_ge(l_stat, count(1, t, 1))
                nc.vector.memset(carrier[:, 0:1], 0.0)
                nc.vector.bn_aggr(mean_var[:, :], stats[:, :]).then_inc(l_aggr, 1)

            def scale_l(t):
                dve.wait_ge(l_root, count(1, t, 1))
                nc.vector.reciprocal(l_rstd[:, :], l_std[:, :]).then_inc(l_inv, 1)
                dve.wait_ge(l_inv, count(1, t, 1))
                nc.vector.tensor_scalar(l_norm[:, :], ps_p[:, 0:USED], mean_var[:, 0:1], l_rstd[:, :], ALU.subtract,
                                        ALU.mult).then_inc(l_scaled, 1)

            def step(t, q):
                tl, ql = at(t, q, 1)
                tm, qm = at(t, q, W_LAG)
                ty, qy = at(t, q, W_LAG + 1)
                if r := due(t, q, COPY_Z):
                    turn_z(r)
                if live(tm):
                    shift_y(tm, qm)
                if live(tl):
                    invert_u(tl, ql)
                if r := due(t, q, LAYER[1]):
                    stats_l(r)
                if live(ty):
                    invert_y(ty, qy)
                if live(tl):
                    scale_u(tl, ql)
                if live(ty):
                    scale_y(ty, qy)
                if live(tm):
                    sum_y(tm, qm)
                if r := due(t, q, LAYER[1]):
                    scale_l(r)
                if first(t):
                    if q == 0:
                        norm_dense()
                        scale_dense()
                    if q == 1:
                        dve.wait_ge(shift_ready, 1)
                        mix_gsi_bsi()
                    if q == 5:
                        scale_wl((0, 1))
                    if q == 6:
                        scale_wl((2,))
                    if q == 7:
                        scale_wl_beside_sums(3)
                if second(t) and q == 1:
                    scale_wl_beside_sums(4)

            place_wsi()
            run(dve, step)


def rows_of_wsi(wsi):
    return np.ascontiguousarray(wsi.T[np.arange(128 * PATTERN) % NF].reshape(PATTERN, 128, P).transpose(1, 0, 2))


def sample_places():
    out = np.zeros((128, PATTERN, BLK), np.float32)
    for tt in range(PATTERN):
        for r in range(128):
            out[r, tt, (128 * tt + r) // NF - 128 * tt // NF] = 1
    return out


def sum_slots():
    out = np.zeros((SUMS, 2, 128), np.float32)
    for n in range(SUMS):
        s, j, i = (n // SLOT_ROW, SQ - 1, n % SLOT_ROW) if n < 4 * SLOT_ROW else (0, SQ - 2, n - 4 * SLOT_ROW)
        assert j > i
        out[n, s // 2, SQ * SQ * (s % 2) + SQ * j + i] = 1
    return out


def pair_rows():
    of = np.full((CHUNKS, 128, 3), -1)
    for c in range(CHUNKS):
        for k in range(128):
            if c < 2:
                j, i1 = 8 * c + k // 16, 16 + k % 16
            else:
                s, j, i1 = k // 64, k // 8 % 8, k % 8
                if c == 2:
                    j, i1 = j + 16 * s, i1 + 8 + 16 * s
                else:
                    j, i1 = j + 8 * (2 * (c - 3) + s), i1 + 8 * (2 * (c - 3) + s)
            if j <= i1:
                of[c, k] = i1 + 1, j, (i1 + 1) * i1 // 2 + j
    return of


def kernel(**inputs):
    import concourse.bacc as _bacc
    from concourse.bass_utils import run_bass_kernel_spmd as _run

    a = {k: np.asarray(v) for k, v in inputs.items()}
    tables = [a[f"tbl_{f}"] for f in range(NF)]
    starts = np.cumsum([0] + [t.shape[0] for t in tables[:-1]]).astype(np.int32)

    def by_row(x):
        return np.ascontiguousarray(x.reshape(ROUNDS * TILES, 128).T)

    def columns(x, n):
        return x.reshape(n, 128).T

    def k_major(x):
        return np.ascontiguousarray(x.reshape(-1, 128, x.shape[1]).transpose(1, 0, 2))

    small = {
        "gs": columns(a["L0_rec_gs"], 1), "gd": columns(a["L0_rec_gd"], 1), "bd": columns(a["L0_rec_bd"], 1),
        "gl": columns(a["L0_rec_gl"][:USED], USED // 128), "bl": columns(a["L0_rec_bl"][:USED], USED // 128),
        "b1": columns(a["b_top1"], H1 // 128), "b2": columns(a["b_top2"], H2 // 128),
        "w3": columns(a["W_top3"][:, 0], H2 // 128),
    }
    of = pair_rows()
    picks = np.zeros((128, 3, CHUNKS, SUMS), np.float32)
    for name, first, own in (("g", a["L0_rec_gsi"], 1), ("b", a["L0_rec_bsi"], 0)):
        with_row0 = np.concatenate([np.full(1, own, first.dtype), first])
        for side in (0, 1):
            small[f"{name}_{'ij'[side]}"] = np.where(of[:, :, side] >= 0, with_row0[of[:, :, side]], 0).astype(first.dtype).T
    wl = np.zeros((128, CHUNKS, MAXD), a["L0_rec_Wl"].dtype)
    for c in range(CHUNKS):
        used = np.flatnonzero(of[c, :, 2] >= 0)
        wl[used, c, :] = a["L0_rec_Wl"].T[of[c, used, 2]]
        picks[used, 0, c, (of[c, used, 0] - 1) % (P + 1)] = 1
        picks[used, 1, c, (of[c, used, 1] - 1) % (P + 1)] = 1
        picks[used, 2, c, SUMS - 1] = 1
    ws_t = np.ascontiguousarray(a["L0_rec_Ws"].T)
    arrays = {
        "tbl": np.concatenate(tables, axis=0),
        "ids": by_row(a["ids"]),
        "base": by_row(np.tile(starts, (B, 1))),
        "ident": np.eye(128, dtype=np.float32),
        "vecs": np.concatenate([small[n] for n in VEC], axis=1),
        "bs_row": np.tile(a["L0_rec_bs"][None, :], (NF, 1)),
        "ws_t": np.concatenate([ws_t, ws_t], axis=0),
        "wsi_rows": rows_of_wsi(a["L0_rec_Wsi"]),
        "places": sample_places(),
        "slots": sum_slots(),
        "dense_t": k_major(np.ascontiguousarray(a["r_dense_t"].T)),
        "wd_t": k_major(np.ascontiguousarray(a["L0_rec_Wd"].T)),
        "wl_chunks": wl,
        "picks": picks,
        "w1": k_major(np.concatenate([a["W_top1"][:USED], a["W_top1"][MAXD:]], axis=0)),
        "w2": k_major(a["W_top2"]),
    }
    nc = _bacc.Bacc("TRN2", target_bir_lowering=False, num_devices=1)
    args = []
    for name, x in arrays.items():
        arrays[name] = np.ascontiguousarray(x)
        args.append(nc.dram_tensor(name, x.shape, mybir.dt.from_np(x.dtype), kind="ExternalInput").ap())
    args.append(nc.dram_tensor("out", (1, B), mybir.dt.float32, kind="ExternalOutput").ap())
    dlrm_tower(nc, *args)
    r = _run(nc, [arrays], core_ids=[0])
    return r.results[0]["out"].reshape(B, 1)
```
